# Optimizing a Trainium2 kernel written in Bass

```python
import numpy as np
import jax
import jax.numpy as jnp

def _softmax(x, axis=-1):
    return jax.nn.softmax(x, axis=axis)

def _gelu(x):
    return jax.nn.gelu(x, approximate=True)

def _silu(x):
    return jax.nn.silu(x)

def _sigmoid(x):
    return jax.nn.sigmoid(x)

def _layernorm(x, axis=-1, eps=1e-05):
    m = jnp.mean(x, axis=axis, keepdims=True)
    v = jnp.var(x, axis=axis, keepdims=True)
    return (x - m) / jnp.sqrt(v + eps)

def _scatter_add(tgt, idx, src, axis=0):
    return tgt.at[idx].add(src)

def _segment_sum(src, seg, n):
    return jax.ops.segment_sum(src, seg, n)
kernel_name = 'mk_adj_resnorm_d4_adj_r2_410b9f'

def setup_inputs(seed: int=0):
    np.random.seed(seed)
    _w = jnp.asarray

    def _rec_inputs():
        import jax
        import jax.numpy as jnp
        _gk = jax.random.key(seed)
        x = -0.0005207 + 1.001 * jax.random.normal(jax.random.fold_in(_gk, 1), (16, 512, 128), jnp.float32)
        _a = jax.random.bernoulli(jax.random.fold_in(_gk, 2), 0.00390625, (16, 512, 512))
        _a = jnp.logical_or(_a, jnp.swapaxes(_a, -1, -2))
        _a = jnp.logical_or(_a, jnp.eye(512, dtype=bool))
        _af = _a.astype(jnp.float32)
        adj = _af
        _nm = jnp.ones((16, 512), dtype=bool)
        nodemask = jnp.where(_nm, 1.0, 0.0).astype(jnp.float32)
        return (x, adj, nodemask)
    x, adj, nodemask = _rec_inputs()

    def _L0_gnn_setup():
        import jax, jax.numpy as jnp
        import numpy as np
        UNITS = 128
        D_FEAT = 128
        B, N = (4, 2048)
        EDGE_PROB = 0.01
        key = jax.random.key(seed)
        k1, k2, k3, k4 = jax.random.split(key, 4)
        x = jax.random.normal(k1, (B, N, D_FEAT), dtype=jnp.float32)
        adj = (jax.random.uniform(k2, (B, N, N)) < EDGE_PROB).astype(jnp.float32)
        W_msg = jax.random.normal(k3, (2 * D_FEAT, UNITS), dtype=jnp.float32) / np.sqrt(2 * D_FEAT).astype(np.float32)
        W_upd = jax.random.normal(k4, (D_FEAT + UNITS, UNITS), dtype=jnp.float32) / np.sqrt(D_FEAT + UNITS).astype(np.float32)
        return {'x': x, 'adj': adj, 'W_msg': W_msg, 'W_upd': W_upd}
    _L0_gnn_all = _L0_gnn_setup()
    _L0_gnn_in = {k: v for k, v in _L0_gnn_all.items() if k in ('W_msg', 'W_upd')}
    del _L0_gnn_all

    def _L1_gnn_setup():
        import jax, jax.numpy as jnp
        import numpy as np
        B, N, C, L = (32, 512, 128, 4)

        def _gru_cell(m, h, w_ih, w_hh, b_ih, b_hh):
            gx = m @ w_ih.T + b_ih
            gh = h @ w_hh.T + b_hh
            xr, xz, xn = jnp.split(gx, 3, axis=-1)
            hr, hz, hn = jnp.split(gh, 3, axis=-1)
            r = jax.nn.sigmoid(xr + hr)
            z = jax.nn.sigmoid(xz + hz)
            n = jnp.tanh(xn + r * hn)
            return (1.0 - z) * n + z * h
        key = jax.random.key(seed)
        ks = jax.random.split(key, 8)
        x = jax.random.normal(ks[0], (B, N, C), dtype=jnp.float32)
        adj = jax.random.randint(ks[1], (B, N, N), 0, 2).astype(jnp.float32)
        mask = jnp.ones((B, N), dtype=jnp.float32)
        s = 1.0 / np.sqrt(C)
        weight = jax.random.uniform(ks[2], (L, C, C), minval=-s, maxval=s, dtype=jnp.float32)
        w_ih = jax.random.uniform(ks[3], (L, 3 * C, C), minval=-s, maxval=s, dtype=jnp.float32)
        w_hh = jax.random.uniform(ks[4], (L, 3 * C, C), minval=-s, maxval=s, dtype=jnp.float32)
        b_ih = jax.random.uniform(ks[5], (L, 3 * C), minval=-s, maxval=s, dtype=jnp.float32)
        b_hh = jax.random.uniform(ks[6], (L, 3 * C), minval=-s, maxval=s, dtype=jnp.float32)
        return {'x': x, 'adj': adj, 'mask': mask, 'weight': weight, 'w_ih': w_ih, 'w_hh': w_hh, 'b_ih': b_ih, 'b_hh': b_hh}
    _L1_gnn_all = _L1_gnn_setup()
    _L1_gnn_in = {k: v for k, v in _L1_gnn_all.items() if k in ('weight', 'w_ih', 'w_hh', 'b_ih', 'b_hh')}
    del _L1_gnn_all

    def _L2_gnn_setup():
        import jax, jax.numpy as jnp
        import numpy as np
        IN_DIM = 128
        OUT_DIM = 128
        NUM_HEADS = 4
        HEAD_DIM = OUT_DIM // NUM_HEADS
        B, N = (8, 1024)
        key = jax.random.key(seed)
        ks = jax.random.split(key, 12)
        s_in = 1.0 / np.sqrt(IN_DIM)
        s_out = 1.0 / np.sqrt(OUT_DIM)
        x = jax.random.normal(ks[0], (B, N, IN_DIM), dtype=jnp.float32)
        adj = jax.random.randint(ks[1], (B, N, N), 0, 2).astype(jnp.float32)
        return {'x': x, 'adj': adj, 'Wq': jax.random.uniform(ks[2], (IN_DIM, OUT_DIM), jnp.float32, -s_in, s_in), 'bq': jax.random.uniform(ks[3], (OUT_DIM,), jnp.float32, -s_in, s_in), 'Wk': jax.random.uniform(ks[4], (IN_DIM, OUT_DIM), jnp.float32, -s_in, s_in), 'bk': jax.random.uniform(ks[5], (OUT_DIM,), jnp.float32, -s_in, s_in), 'Wv': jax.random.uniform(ks[6], (IN_DIM, OUT_DIM), jnp.float32, -s_in, s_in), 'bv': jax.random.uniform(ks[7], (OUT_DIM,), jnp.float32, -s_in, s_in), 'Wo': jax.random.uniform(ks[8], (OUT_DIM, OUT_DIM), jnp.float32, -s_out, s_out), 'bo': jax.random.uniform(ks[9], (OUT_DIM,), jnp.float32, -s_out, s_out)}
    _L2_gnn_all = _L2_gnn_setup()
    _L2_gnn_in = {k: v for k, v in _L2_gnn_all.items() if k in ('Wq', 'bq', 'Wk', 'bk', 'Wv', 'bv', 'Wo', 'bo')}
    del _L2_gnn_all

    def _L3_gnn_setup():
        import jax, jax.numpy as jnp
        import numpy as np
        B, N, F_IN, F_OUT = (8, 2048, 128, 128)
        key = jax.random.key(seed)
        k1, k2, k3, k4 = jax.random.split(key, 4)
        stdv = 1.0 / np.sqrt(F_OUT)
        inputs = jax.random.normal(k1, (B, N, F_IN), dtype=jnp.float32)
        adj = jax.random.uniform(k2, (B, N, N), dtype=jnp.float32)
        weight = jax.random.uniform(k3, (F_IN, F_OUT), minval=-stdv, maxval=stdv, dtype=jnp.float32)
        bias = jax.random.uniform(k4, (F_OUT,), minval=-stdv, maxval=stdv, dtype=jnp.float32)
        return {'input': inputs, 'adj': adj, 'weight': weight, 'bias': bias}
    _L3_gnn_all = _L3_gnn_setup()
    _L3_gnn_in = {k: v for k, v in _L3_gnn_all.items() if k in ('weight', 'bias')}
    del _L3_gnn_all
    return {'x': x, 'adj': adj, 'nodemask': nodemask, 'L0_gnn_W_msg': _L0_gnn_in['W_msg'], 'L0_gnn_W_upd': _L0_gnn_in['W_upd'], 'L1_gnn_weight': _L1_gnn_in['weight'], 'L1_gnn_w_ih': _L1_gnn_in['w_ih'], 'L1_gnn_w_hh': _L1_gnn_in['w_hh'], 'L1_gnn_b_ih': _L1_gnn_in['b_ih'], 'L1_gnn_b_hh': _L1_gnn_in['b_hh'], 'L2_gnn_Wq': _L2_gnn_in['Wq'], 'L2_gnn_bq': _L2_gnn_in['bq'], 'L2_gnn_Wk': _L2_gnn_in['Wk'], 'L2_gnn_bk': _L2_gnn_in['bk'], 'L2_gnn_Wv': _L2_gnn_in['Wv'], 'L2_gnn_bv': _L2_gnn_in['bv'], 'L2_gnn_Wo': _L2_gnn_in['Wo'], 'L2_gnn_bo': _L2_gnn_in['bo'], 'L3_gnn_weight': _L3_gnn_in['weight'], 'L3_gnn_bias': _L3_gnn_in['bias']}

def reference(x, adj, nodemask, L0_gnn_W_msg, L0_gnn_W_upd, L1_gnn_weight, L1_gnn_w_ih, L1_gnn_w_hh, L1_gnn_b_ih, L1_gnn_b_hh, L2_gnn_Wq, L2_gnn_bq, L2_gnn_Wk, L2_gnn_bk, L2_gnn_Wv, L2_gnn_bv, L2_gnn_Wo, L2_gnn_bo, L3_gnn_weight, L3_gnn_bias):
    import jax
    import jax.numpy as jnp

    def _L0_gnn_ref(x, adj, W_msg, W_upd):
        import jax, jax.numpy as jnp
        import numpy as np
        UNITS = 128
        D_FEAT = 128
        B, N = (4, 2048)
        EDGE_PROB = 0.01
        d = x.shape[-1]
        Ws, Wr = (W_msg[:d], W_msg[d:])
        xs = x @ Ws
        xr = x @ Wr
        deg = jnp.einsum('bsr->br', adj)[..., None]
        snd_sum = jnp.einsum('bsr,bsu->bru', adj, xs)
        messages = jnp.where(deg > 0, snd_sum / jnp.maximum(deg, 1.0) + xr, 0.0)
        return jnp.concatenate([x, messages], axis=-1) @ W_upd

    def _L1_gnn_ref(x, adj, mask, weight, w_ih, w_hh, b_ih, b_hh):
        import jax, jax.numpy as jnp
        import numpy as np
        B, N, C, L = (32, 512, 128, 4)

        def _gru_cell(m, h, w_ih, w_hh, b_ih, b_hh):
            gx = m @ w_ih.T + b_ih
            gh = h @ w_hh.T + b_hh
            xr, xz, xn = jnp.split(gx, 3, axis=-1)
            hr, hz, hn = jnp.split(gh, 3, axis=-1)
            r = jax.nn.sigmoid(xr + hr)
            z = jax.nn.sigmoid(xz + hz)
            n = jnp.tanh(xn + r * hn)
            return (1.0 - z) * n + z * h
        h = x
        for i in range(L):
            hw = jnp.einsum('bnc,cd->bnd', h, weight[i])
            m = jnp.einsum('bjn,bjd->bnd', adj, hw)
            h = _gru_cell(m, h, w_ih[i], w_hh[i], b_ih[i], b_hh[i])
        return h * mask[:, :, None]

    def _L2_gnn_ref(x, adj, Wq, bq, Wk, bk, Wv, bv, Wo, bo):
        import jax, jax.numpy as jnp
        import numpy as np
        IN_DIM = 128
        OUT_DIM = 128
        NUM_HEADS = 4
        HEAD_DIM = OUT_DIM // NUM_HEADS
        B, N = (8, 1024)
        Bs, Ns, _ = x.shape
        scale = jnp.sqrt(jnp.asarray(HEAD_DIM, dtype=x.dtype))
        Q = (x @ Wq + bq).reshape(Bs, Ns, NUM_HEADS, HEAD_DIM)
        K = (x @ Wk + bk).reshape(Bs, Ns, NUM_HEADS, HEAD_DIM)
        V = (x @ Wv + bv).reshape(Bs, Ns, NUM_HEADS, HEAD_DIM)
        scores = jnp.einsum('bnhd,bmhd->bhnm', Q, K) / scale
        scores = scores + (1.0 - adj[:, None, :, :]) * -1000000000.0
        attn = jax.nn.softmax(scores, axis=-1)
        out = jnp.einsum('bhnm,bmhd->bnhd', attn, V).reshape(Bs, Ns, OUT_DIM)
        return out @ Wo + bo

    def _L3_gnn_ref(input, adj, weight, bias):
        import jax, jax.numpy as jnp
        import numpy as np
        B, N, F_IN, F_OUT = (8, 2048, 128, 128)
        support = jnp.einsum('bnf,fo->bno', input, weight)
        n = adj.shape[-1]
        adj_post = adj + jnp.eye(n, dtype=adj.dtype)
        deg_inv_sqrt = jnp.sum(jnp.abs(adj_post), axis=-1) ** (-0.5)
        norm_adj = adj_post * deg_inv_sqrt[:, :, None] * deg_inv_sqrt[:, None, :]
        out = jnp.einsum('bnm,bmo->bno', norm_adj, support)
        return out + bias
    x = _layernorm(x + _L0_gnn_ref(x, adj, L0_gnn_W_msg, L0_gnn_W_upd), axis=-1)
    x = _layernorm(x + _L1_gnn_ref(x, adj, nodemask, L1_gnn_weight, L1_gnn_w_ih, L1_gnn_w_hh, L1_gnn_b_ih, L1_gnn_b_hh), axis=-1)
    x = _layernorm(x + _L2_gnn_ref(x, adj, L2_gnn_Wq, L2_gnn_bq, L2_gnn_Wk, L2_gnn_bk, L2_gnn_Wv, L2_gnn_bv, L2_gnn_Wo, L2_gnn_bo), axis=-1)
    x = _layernorm(x + _L3_gnn_ref(x, adj, L3_gnn_weight, L3_gnn_bias), axis=-1)
    return x

_drawn_inputs = setup_inputs


def setup_inputs(seed=0):
    import zlib

    import numpy as np

    out = dict(_drawn_inputs(seed))
    spreads = {}
    factors = {'L2_gnn_bq': 8.0, 'L2_gnn_bk': 8.0}
    for name, (base, spread) in spreads.items():
        noise = np.random.default_rng([zlib.crc32(name.encode()), seed]).standard_normal(out[name].shape)
        drawn = base * np.exp(spread * noise) if base else spread * noise
        out[name] = jnp.asarray(drawn.astype(out[name].dtype))
    for name, factor in factors.items():
        out[name] = (out[name] * factor).astype(out[name].dtype)
    return out
```

```python
from contextlib import ExitStack

import concourse.bass as bass
from concourse import mybir

F32 = mybir.dt.float32
F32R = mybir.dt.float32r
I32 = mybir.dt.int32
ALU = mybir.AluOpType
ACT = mybir.ActivationFunctionType
AX = mybir.AxisListType

GRAPHS, NODES, FEATS = 16, 512, 128
P = 128
CHUNKS = NODES // P
LAYERS = 4
HEADS = 4
HEAD = FEATS // HEADS
UNITS = CHUNKS * HEADS
STRANDS = 2
TURNS = GRAPHS // STRANDS
LN_EPS = 1e-5
MASK = 1e9
SCORE_SCALE = float(HEAD) ** -0.5
DMA = 16

NORM1, NORM2, DEGREE, NORM3, NORM4 = range(5)
ROOTS = 5
NEWTON_ROUNDS = 3
NEWTON_STEPS = 4 * NEWTON_ROUNDS
SEED = 0x5F3759DF
ROOT_TICKS = [4, 4, 2, 4, 4]
TICK_BASE = [sum(ROOT_TICKS[:k]) for k in range(ROOTS)]
TICKS = sum(ROOT_TICKS)
Q_LOW, Q_HIGH, K_HIGH, K_LOW = range(4)
PRODUCTS = [(Q_HIGH, K_HIGH), (Q_HIGH, K_LOW), (Q_LOW, K_HIGH), (Q_LOW, K_LOW)]
HIGH, LOW = (Q_HIGH, K_HIGH), (Q_LOW, K_LOW)
STACKS = len(PRODUCTS) * HEADS

FIRST = [("turn1",)]
for i in range(LAYERS):
    FIRST += [("aggregate", i, 0), ("aggregate", i, 1), ("gates_state", i), ("gates_sum", i), ("update", i),
              ("turn_state", i)]
FIRST += [("norm2",), ("apply2",)]

LAYER0 = [("project",), ("message",), ("norm1",), ("apply1",)]
SECOND = [("turn2",), ("mask",), ("qkv",), ("degree",), ("score", 0), ("score", 1)]
for u in range(UNITS):
    SECOND += [("weights", u)]
    if u + 2 < UNITS:
        SECOND += [("score", u + 2)]
    if u % HEADS == 1 and u > HEADS:
        SECOND += [("mix", u // HEADS - 1)]
SECOND += [("mix", CHUNKS - 1), ("merge",), ("apply3",), ("turn3",), ("support",), ("spread",), ("apply4",)]
SECOND += [("next", name) for name, in LAYER0]

BEHIND = [
    0,
    2, 2, 0, 0, 1, 0,
    2, 3, 4, 3, 8, 0,
    2, 3, 3, 3, 7, 0,
    0, 1, 1, 3, 3, 0,
    4, 2,
]


def phase_order():
    order, at = [], 0
    for step, n in zip(FIRST, BEHIND):
        order += [(0, step)] + [(1, x) for x in SECOND[at:at + n]]
        at += n
    return order + [(1, x) for x in SECOND[at:]]


PHASE = phase_order()


def walk(steps, first, second):
    for half, (name, *arg) in PHASE:
        if first is None and half == 0 or second is None and half == 1:
            continue
        s, t = (first, second)[half]
        if name == "next":
            if isinstance(t, int) and t + 1 == TURNS:
                continue
            t, name, arg = t + 1, arg[0], []
        if name in steps:
            steps[name](s, t, *arg)


def run_phases(engine, steps):
    for name, in LAYER0:
        for s in range(STRANDS):
            if name in steps:
                steps[name](s, 0)
    walk(steps, (0, 0), None)
    with engine.Fori(0, TURNS - 1) as t:
        walk(steps, (1, t), (0, t))
        walk(steps, (0, t + 1), (1, t))
    walk(steps, (1, TURNS - 1), (0, TURNS - 1))
    walk(steps, None, (1, TURNS - 1))


def graph_layers(nc, x_columns, adj, adj_t, node_mask, w_msg_t, w_upd, weight_t, w_ih_t, w_hh_t, b_ih, b_hh,
                 wq, bq, wk, bk, wv, bv, wo, bo, w3, b3, out):
    ctx = ExitStack()
    with ctx:
        def sb(name, shape, dt=F32):
            return ctx.enter_context(nc.sbuf_tensor(name, shape, dt))

        def pair(name, shape, dt=F32):
            return [sb(f"{name}{s}", shape, dt) for s in range(STRANDS)]

        def sem(name):
            return ctx.enter_context(nc.semaphore(name))

        def sems(name):
            return [sem(f"{name}{s}") for s in range(STRANDS)]

        ident = sb("ident", [P, P])
        c15 = sb("c15", [P, CHUNKS])
        wmt = sb("wmt", [P, 2 * FEATS])
        wu = sb("wu", [P, 2, FEATS])
        w0 = sb("w0", [P, 3, FEATS])
        wt = sb("wt", [P, LAYERS, FEATS])
        wih = sb("wih", [P, LAYERS, 3 * FEATS])
        wwi = sb("wwi", [P, LAYERS, 3 * FEATS])
        whh = sb("whh", [P, LAYERS, 3 * FEATS])
        bi = sb("bi", [P, LAYERS, 3])
        bh = sb("bh", [P, LAYERS, 3])
        brz = sb("brz", [P, LAYERS, 3])
        bhn = sb("bhn", [P, LAYERS, 1])
        wqk = sb("wqk", [P, 2, FEATS])
        bqk = sb("bqk", [P, 2])
        wqn = sb("wqn", [P, FEATS])
        bqn = sb("bqn", [P, 1])
        wv_s = sb("wv_s", [P, FEATS])
        wo_s = sb("wo_s", [P, FEATS])
        w3_s = sb("w3_s", [P, FEATS])
        bv_s = sb("bv_s", [P, FEATS])
        bo_s = sb("bo_s", [P, FEATS])
        b3_s = sb("b3_s", [P, FEATS])
        ones = sb("ones", [P, HEAD])

        adj_s = pair("adj_s", [P, CHUNKS, NODES])
        adjt_s = pair("adjt_s", [P, CHUNKS, NODES])
        xcol = pair("xcol", [P, NODES])
        nmask = pair("nmask", [P, CHUNKS])
        sent = pair("sent", [P, CHUNKS, FEATS + 1])
        deg = pair("deg", [P, CHUNKS])
        has = pair("has", [P, CHUNKS])
        inv = pair("inv", [P, CHUNKS])
        minv = pair("minv", [P, CHUNKS])
        y = pair("y", [P, CHUNKS, FEATS])
        y2 = pair("y2", [P, CHUNKS, FEATS])
        stats = pair("stats", [P, CHUNKS, 6])
        mv = pair("mv", [P, CHUNKS, 2])
        ve = pair("ve", [P, CHUNKS])
        vh = pair("vh", [P, CHUNKS])
        bits = pair("bits", [P, CHUNKS], I32)
        root = pair("root", [P, CHUNKS])
        sq = pair("sq", [P, CHUNKS])
        d3 = pair("d3", [P, CHUNKS])
        x1 = pair("x1", [P, CHUNKS, FEATS])
        state = pair("state", [P, NODES])
        state_rows = pair("state_rows", [P, CHUNKS, FEATS])
        aggr = pair("aggr", [P, NODES])
        cand = pair("cand", [P, NODES])
        reset = pair("reset", [P, NODES])
        keep = pair("keep", [P, NODES])
        new = pair("new", [P, NODES])
        diff = pair("diff", [P, NODES])
        x2 = pair("x2", [P, CHUNKS, FEATS])
        x3 = pair("x3", [P, CHUNKS, FEATS])
        xb = pair("xb", [P, CHUNKS, FEATS])
        xturn = pair("xturn", [P, NODES])
        vals = pair("vals", [P, CHUNKS, FEATS])
        low = pair("low", [P, UNITS])
        rsum = pair("rsum", [P, P])
        ocol = pair("ocol", [P, NODES])
        supp = pair("supp", [P, CHUNKS, FEATS])
        y4 = pair("y4", [P, CHUNKS, FEATS])

        far = sb("far", [P, CHUNKS, NODES])
        parts = sb("parts", [P, 4, NODES], F32R)
        stack = sb("stack", [P, 2, HEADS, NODES], F32R)
        masked = [sb(f"masked{b}", [P, NODES]) for b in range(2)]
        prob = [sb(f"prob{b}", [P, NODES]) for b in range(2)]
        prob_t = [sb(f"prob_t{b}", [P, CHUNKS, HEADS, P]) for b in range(2)]

        bank = [[ctx.enter_context(nc.psum_tensor(f"bank{s}{b}", [P, NODES], F32)) for b in range(4)]
                for s in range(STRANDS)]

        def chunks(ap):
            return ap.rearrange("p (c f) -> p c f", c=CHUNKS)

        def spread(ap, n=FEATS):
            return ap.unsqueeze(2).broadcast_to([P, ap.shape[1], n])

        def rows_of(ap):
            return ap.unsqueeze(1).broadcast_to([P, CHUNKS, FEATS])

        w_loaded = sem("w_loaded")
        bias_summed = sem("bias_summed")
        waited = sem("waited")
        ident_zeroed = sem("ident_zeroed")
        consts_ready = sem("consts_ready")
        fused_done = sem("fused_done")
        w_ready = sem("w_ready")
        x_loaded = sems("x_loaded")
        adj_loaded = sems("adj_loaded")
        adjt_loaded = sems("adjt_loaded")
        projected = sems("projected")
        sent_ready = sems("sent_ready")
        messages_done = sems("messages_done")
        combined = sems("combined")
        norm_tick = sems("norm_tick")
        seeded = sems("seeded")
        newton = sems("newton")
        x1_ready = sems("x1_ready")
        x1_turned = sems("x1_turned")
        state0_ready = sems("state0_ready")
        aggregated = sems("aggregated")
        aggr_ready = sems("aggr_ready")
        hn_done = sems("hn_done")
        r_done = sems("r_done")
        xn_done = sems("xn_done")
        z_done = sems("z_done")
        hn_ready = sems("hn_ready")
        reset_ready = sems("reset_ready")
        gated = sems("gated")
        cand_ready = sems("cand_ready")
        new_ready = sems("new_ready")
        keep_ready = sems("keep_ready")
        diff_ready = sems("diff_ready")
        state_ready = sems("state_ready")
        state_turned = sems("state_turned")
        rows_ready = sems("rows_ready")
        y_ready = sems("y_ready")
        x2_ready = sems("x2_ready")
        x2_turned = sems("x2_turned")
        x2col_ready = sems("x2col_ready")
        qkv_done = sems("qkv_done")
        high_ready = sems("high_ready")
        low_ready = sems("low_ready")
        vals_ready = sems("vals_ready")
        stacked = sems("stacked")
        far_ready = sems("far_ready")
        self_added = sems("self_added")
        selft_added = sems("selft_added")
        deg3_ready = sems("deg3_ready")
        d3_ready = sems("d3_ready")
        scored = sems("scored")
        masked_ready = sems("masked_ready")
        prob_ready = sems("prob_ready")
        prob_turned = sems("prob_turned")
        probt_ready = sems("probt_ready")
        mixed = sems("mixed")
        rsum_ready = sems("rsum_ready")
        ocol_ready = sems("ocol_ready")
        xb_ready = sems("xb_ready")
        merged = sems("merged")
        x3_ready = sems("x3_ready")
        x3_turned = sems("x3_turned")
        x3col_ready = sems("x3col_ready")
        supported = sems("supported")
        supp_ready = sems("supp_ready")
        spread_done = sems("spread_done")
        y4_ready = sems("y4_ready")
        stored = sems("stored")

        WEIGHT_LOADS = 17
        block = ctx.enter_context(nc.Block())

        @block.sync
        def _(sp):
            def load_x(s, t):
                sp.dma_start(xcol[s][:, :], x_columns[t * STRANDS + s]).then_inc(x_loaded[s], DMA)
                sp.dma_start(nmask[s][:, :], node_mask[t * STRANDS + s]
                             ).then_inc(x_loaded[s], DMA)

            def load_adj(s, t):
                sp.dma_start(adj_s[s][:, :, :], adj[t * STRANDS + s].rearrange("(c p) m -> p c m", p=P)
                             ).then_inc(adj_loaded[s], DMA)

            def load_adjt(s, t):
                sp.dma_start(adjt_s[s][:, :, :], adj_t[t * STRANDS + s].rearrange("(c p) m -> p c m", p=P)
                             ).then_inc(adjt_loaded[s], DMA)

            load_x(0, 0)
            for tile, src in (
                (wmt[:, :], w_msg_t), (wu[:, :, :], w_upd.rearrange("(h k) n -> k h n", h=2)),
            ):
                sp.dma_start(tile, src).then_inc(w_loaded, DMA)
            load_adj(0, 0)
            for tile, src in (
                (wt[:, :, :], weight_t.rearrange("l d c -> d l c")), (wih[:, :, :], w_ih_t.rearrange("l d g -> d l g")),
                (whh[:, :, :], w_hh_t.rearrange("l d g -> d l g")),
                (bi[:, :, :], b_ih), (bh[:, :, :], b_hh),
                (wqk[:, 0, :], wq), (wqk[:, 1, :], wk),
                (bqk[:, 0:1], bq), (bqk[:, 1:2], bk),
                (wv_s[:, :], wv), (wo_s[:, :], wo), (w3_s[:, :], w3),
                (bv_s[:, :], bv.partition_broadcast(P)), (bo_s[:, :], bo.partition_broadcast(P)),
                (b3_s[:, :], b3.partition_broadcast(P)),
            ):
                sp.dma_start(tile, src).then_inc(w_loaded, DMA)
            load_adjt(0, 0)
            load_x(1, 0)
            load_adj(1, 0)
            load_adjt(1, 0)

            def qkv(s, t):
                sp.wait_ge(high_ready[s], t * 2 + 2)
                sp.wait_ge(low_ready[s], t * 2 + 2)
                for h in range(HEADS):
                    rows = slice(HEAD * h, HEAD * h + HEAD)
                    for quadrant, (q, k) in enumerate(PRODUCTS):
                        sp.dma_start(stack[HEAD * quadrant:HEAD * quadrant + HEAD, :, h, :].bitcast(F32),
                                     parts[rows, q:k + 1:k - q, :].bitcast(F32)).then_inc(stacked[s], DMA)

            def more(t):
                return not isinstance(t, int) or t + 1 < TURNS

            def degree(s, t):
                if more(t):
                    sp.wait_ge(x2_ready[s], t + 1)
                    load_x(s, t + 1)
                    sp.wait_ge(deg3_ready[s], t + 1)
                    load_adj(s, t + 1)

            def apply4(s, t):
                if more(t):
                    sp.wait_ge(spread_done[s], t + 1)
                    load_adjt(s, t + 1)
                sp.wait_ge(y4_ready[s], t + 1)
                sp.dma_start(out[t * STRANDS + s].rearrange("(c p) f -> p c f", p=P), y4[s][:, :, :]
                             ).then_inc(stored[s], DMA)

            run_phases(sp, {"qkv": qkv, "degree": degree, "apply4": apply4})
            for s in range(STRANDS):
                sp.wait_ge(stored[s], DMA * TURNS + DMA)

        @block.tensor
        def _(pe):
            pe.wait_ge(consts_ready, 4)
            pe.wait_ge(w_loaded, DMA * WEIGHT_LOADS)
            for h in range(2):
                pe.matmul(bank[1][0][:, h * FEATS:h * FEATS + FEATS], wmt[:, h * FEATS:h * FEATS + FEATS],
                          wu[:, 1, :], start=(h == 0), stop=(h == 1), skip_group_check=True)
            for i in range(LAYERS):
                last = pe.matmul(bank[0][i][:, 0:3 * FEATS], wt[:, i, :], wih[:, i, :], start=True, stop=True)
            last.then_inc(fused_done, 1)
            pe.wait_ge(w_ready, 8)

            def project(s, t):
                pe.wait_ge(x_loaded[s], t * 2 * DMA + 2 * DMA)
                pe.wait_ge(y_ready[s], t * 5 + 1)
                for part in range(3):
                    for c in range(CHUNKS):
                        mm = pe.matmul(bank[s][part][:, c * P:c * P + P], xcol[s][:, c * P:c * P + P],
                                       w0[:, part, :], start=(c == 0), stop=(c == CHUNKS - 1),
                                       skip_group_check=True)
                    if part != 1:
                        mm.then_inc(projected[s], 1)

            def message(s, t):
                pe.wait_ge(sent_ready[s], t + 1)
                pe.wait_ge(adj_loaded[s], t * DMA + DMA)
                W = FEATS + 1
                for r in range(CHUNKS):
                    dst = bank[s][3][:, r * W:r * W + W] if r < 3 else bank[s][0][:, 0:W]
                    for c in range(CHUNKS):
                        mm = pe.matmul(dst, adj_s[s][:, c, r * P:r * P + P], sent[s][:, c, :],
                                       start=(c == 0), stop=(c == CHUNKS - 1), skip_group_check=True)
                mm.then_inc(messages_done[s], 1)

            def turn(dst, rows):
                for c in range(CHUNKS):
                    mm = pe.transpose(dst[:, c * P:c * P + P], rows(c), ident[:, :])
                return mm

            def turn1(s, t):
                pe.wait_ge(x1_ready[s], t + 1)
                turn(bank[s][1], lambda c: x1[s][:, c, :]).then_inc(x1_turned[s], 1)

            def aggregate(s, t, i, half):
                if i == 0:
                    pe.wait_ge(x1_ready[s], t + 1)
                else:
                    pe.wait_ge(rows_ready[s], t * (LAYERS - 1) + i)
                rows = x1[s] if i == 0 else state_rows[s]
                for c in range(half * CHUNKS // 2, (half + 1) * CHUNKS // 2):
                    mm = pe.matmul(bank[s][0][:, :], rows[:, c, :], adj_s[s][:, c, :],
                                   start=(c == 0), stop=(c == CHUNKS - 1))
                if half:
                    mm.then_inc(aggregated[s], 1)

            R, Z, N = (slice(g * FEATS, g * FEATS + FEATS) for g in range(3))

            def gates_state(s, t, i):
                if i == 0:
                    pe.wait_ge(state0_ready[s], t + 1)
                pe.matmul(bank[s][3][:, :], whh[:, i, N], state[s][:, :], start=True, stop=True
                          ).then_inc(hn_done[s], 1)
                pe.matmul(bank[s][1][:, :], whh[:, i, R], state[s][:, :], start=True, stop=False)
                pe.matmul(bank[s][2][:, :], whh[:, i, Z], state[s][:, :], start=True, stop=False)

            def gates_sum(s, t, i):
                pe.wait_ge(aggr_ready[s], t * LAYERS + i + 1)
                pe.matmul(bank[s][1][:, :], wwi[:, i, R], aggr[s][:, :], start=False, stop=True
                          ).then_inc(r_done[s], 1)
                pe.matmul(bank[s][0][:, :], wwi[:, i, N], aggr[s][:, :], start=True, stop=True
                          ).then_inc(xn_done[s], 1)
                pe.matmul(bank[s][2][:, :], wwi[:, i, Z], aggr[s][:, :], start=False, stop=True
                          ).then_inc(z_done[s], 1)

            def turn_state(s, t, i):
                pe.wait_ge(state_ready[s], t * LAYERS + i + 1)
                turn(bank[s][1], lambda c: state[s][:, c * P:c * P + P]).then_inc(state_turned[s], 1)

            def turn2(s, t):
                pe.wait_ge(x2_ready[s], t + 1)
                turn(bank[s][0], lambda c: x2[s][:, c, :]).then_inc(x2_turned[s], 1)

            def qkv(s, t):
                pe.wait_ge(x2col_ready[s], t + 1)
                pe.matmul(bank[s][1][:, :], wqn[:, :], xturn[s][:, :], start=True, stop=True
                          ).then_inc(qkv_done[s], 1)
                pe.matmul(bank[s][2][:, :], wqk[:, 1, :], xturn[s][:, :], start=True, stop=True
                          ).then_inc(qkv_done[s], 1)
                for c in range(CHUNKS):
                    mm = pe.matmul(bank[s][3][:, c * P:c * P + P], xturn[s][:, c * P:c * P + P], wv_s[:, :],
                                   start=(c == 0), stop=(c == CHUNKS - 1), skip_group_check=True)
                mm.then_inc(qkv_done[s], 1)

            def score(s, t, u):
                c, h = u // HEADS, u % HEADS
                if u == 0:
                    pe.wait_ge(stacked[s], t * DMA * STACKS + DMA * STACKS)
                if u >= 2:
                    pe.wait_ge(masked_ready[s], t * UNITS + u - 1)
                pe.matmul(bank[s][1 + u % 2][:, :], stack[:, 0, h, c * P:c * P + P], stack[:, 1, h, :],
                          start=True, stop=True).then_inc(scored[s], 1)

            def weights(s, t, u):
                if u == 0:
                    pe.wait_ge(vals_ready[s], t + 1)
                else:
                    pe.wait_ge(probt_ready[s], t * UNITS + u)
                pe.wait_ge(prob_ready[s], t * UNITS + u + 1)
                turn(bank[s][3], lambda m: prob[u % 2][:, m * P:m * P + P]).then_inc(prob_turned[s], 1)

            def mix(s, t, c):
                pe.wait_ge(probt_ready[s], t * UNITS + HEADS * c + HEADS)
                if c:
                    pe.wait_ge(ocol_ready[s], t * CHUNKS + c)
                for part in range(2):
                    for m in range(CHUNKS):
                        for h in range(HEADS):
                            rows = slice(HEAD * h, HEAD * h + HEAD)
                            lhs = vals[s][:, m, rows] if part == 0 else ones[:, :]
                            mm = pe.matmul(bank[s][0][rows, part * P:part * P + P], lhs,
                                           prob_t[c % 2][:, m, h, :], start=(m == 0), stop=(m == CHUNKS - 1),
                                           skip_group_check=True)
                mm.then_inc(mixed[s], 1)

            def merge(s, t):
                pe.wait_ge(ocol_ready[s], t * CHUNKS + CHUNKS)
                pe.wait_ge(masked_ready[s], t * UNITS + UNITS)
                for c in range(CHUNKS):
                    mm = pe.matmul(bank[s][1][:, c * P:c * P + P], ocol[s][:, c * P:c * P + P], wo_s[:, :],
                                   start=(c == 0), stop=(c == CHUNKS - 1), skip_group_check=True)
                mm.then_inc(merged[s], 1)

            def turn3(s, t):
                pe.wait_ge(x3_ready[s], t + 1)
                turn(bank[s][0], lambda c: x3[s][:, c, :]).then_inc(x3_turned[s], 1)

            def support(s, t):
                pe.wait_ge(x3col_ready[s], t + 1)
                for c in range(CHUNKS):
                    mm = pe.matmul(bank[s][2][:, c * P:c * P + P], xturn[s][:, c * P:c * P + P], w3_s[:, :],
                                   start=(c == 0), stop=(c == CHUNKS - 1), skip_group_check=True)
                mm.then_inc(supported[s], 1)

            def spread3(s, t):
                pe.wait_ge(selft_added[s], t + 1)
                pe.wait_ge(supp_ready[s], t + 1)
                for n in range(CHUNKS):
                    for m in range(CHUNKS):
                        mm = pe.matmul(bank[s][3][:, n * P:n * P + P], adjt_s[s][:, m, n * P:n * P + P],
                                       supp[s][:, m, :], start=(m == 0), stop=(m == CHUNKS - 1),
                                       skip_group_check=True)
                mm.then_inc(spread_done[s], 1)

            run_phases(pe, {
                "project": project, "message": message, "turn1": turn1, "aggregate": aggregate,
                "gates_state": gates_state, "gates_sum": gates_sum, "turn_state": turn_state, "turn2": turn2, "qkv": qkv, "score": score, "weights": weights,
                "mix": mix, "merge": merge, "turn3": turn3, "support": support, "spread": spread3,
            })

        @block.scalar
        def _(act):
            act.wait_ge(fused_done, 1)
            for i in range(LAYERS):
                act.copy(wwi[:, i, :], bank[0][i][:, 0:3 * FEATS]).then_inc(w_ready, 1)

            def project(s, t):
                act.wait_ge(projected[s], t * 2 + 1)
                act.copy(sent[s][:, :, 0:FEATS], chunks(bank[s][0][:, :])).then_inc(sent_ready[s], 1)

            def turn1(s, t):
                act.wait_ge(x1_turned[s], t + 1)
                act.copy(state[s][:, :], bank[s][1][:, :]).then_inc(state0_ready[s], 1)

            def aggregate(s, t, i, half):
                if half == 0:
                    return
                act.wait_ge(aggregated[s], t * LAYERS + i + 1)
                act.copy(aggr[s][:, :], bank[s][0][:, :]).then_inc(aggr_ready[s], 1)

            def gates_state(s, t, i):
                act.wait_ge(hn_done[s], t * LAYERS + i + 1)
                act.activation(cand[s][:, :], bank[s][3][:, :], ACT.Identity, bias=bhn[:, i, :], scale=0.5
                               ).then_inc(hn_ready[s], 1)

            def gates_sum(s, t, i):
                act.wait_ge(r_done[s], t * LAYERS + i + 1)
                act.activation(reset[s][:, :], bank[s][1][:, :], ACT.Tanh, bias=brz[:, i, 0:1], scale=0.5
                               ).then_inc(reset_ready[s], 1)

            def update(s, t, i):
                act.wait_ge(cand_ready[s], t * LAYERS + i + 1)
                act.activation(new[s][:, :], cand[s][:, :], ACT.Tanh, bias=bi[:, i, 2:3], scale=1.0
                               ).then_inc(new_ready[s], 1)
                act.wait_ge(z_done[s], t * LAYERS + i + 1)
                act.activation(keep[s][:, :], bank[s][2][:, :], ACT.Tanh, bias=brz[:, i, 1:2], scale=0.5
                               ).then_inc(keep_ready[s], 1)

            def turn_state(s, t, i):
                if i < LAYERS - 1:
                    act.wait_ge(state_turned[s], t * LAYERS + i + 1)
                    act.copy(state_rows[s][:, :, :], chunks(bank[s][1][:, :])).then_inc(rows_ready[s], 1)

            def turn2(s, t):
                act.wait_ge(x2_turned[s], t + 1)
                act.copy(xturn[s][:, :], bank[s][0][:, :]).then_inc(x2col_ready[s], 1)

            def qkv(s, t):
                for tensor, bias in ((0, bqn[:, 0:1]), (1, bqk[:, 1:2])):
                    act.wait_ge(qkv_done[s], t * 3 + tensor + 1)
                    act.activation(parts[:, HIGH[tensor], :], bank[s][1 + tensor][:, :], ACT.Identity,
                                   bias=bias, scale=1.0).then_inc(high_ready[s], 1)

            def degree(s, t):
                act.wait_ge(self_added[s], t + 1)
                for c in range(CHUNKS):
                    a = act.activation(adj_s[s][:, c, :], adj_s[s][:, c, :], ACT.Abs, accum_out=deg[s][:, c:c + 1])
                a.then_inc(deg3_ready[s], 1)

            def score(s, t, u):
                act.wait_ge(masked_ready[s], t * UNITS + u + 1)
                if u >= 2:
                    act.wait_ge(prob_turned[s], t * UNITS + u - 1)
                act.activation(prob[u % 2][:, :], masked[u % 2][:, :], ACT.Exp, bias=low[s][:, u:u + 1],
                               scale=-1.0).then_inc(prob_ready[s], 1)

            def weights(s, t, u):
                c, h = u // HEADS, u % HEADS
                act.wait_ge(prob_turned[s], t * UNITS + u + 1)
                if c >= 2:
                    act.wait_ge(mixed[s], t * CHUNKS + c - 1)
                act.copy(prob_t[c % 2][:, :, h, :], chunks(bank[s][3][:, :])).then_inc(probt_ready[s], 1)

            def turn3(s, t):
                act.wait_ge(x3_turned[s], t + 1)
                act.copy(xturn[s][:, :], bank[s][0][:, :]).then_inc(x3col_ready[s], 1)

            run_phases(act, {
                "project": project, "turn1": turn1, "aggregate": aggregate, "gates_state": gates_state, "gates_sum": gates_sum,
                "update": update, "turn_state": turn_state, "turn2": turn2, "qkv": qkv, "degree": degree, "score": score,
                "weights": weights, "turn3": turn3,
            })

        @block.vector
        def _(dve):
            for s in range(STRANDS):
                dve.sem_inc(y_ready[s], 1)
                dve.sem_inc(stored[s], DMA)
                dve.memset(sent[s][:, :, FEATS:FEATS + 1], 1.0).then_inc(consts_ready, 1)
            dve.memset(ones[:, :], 1.0).then_inc(consts_ready, 1)
            dve.wait_ge(w_loaded, DMA * WEIGHT_LOADS)
            dve.tensor_tensor(brz[:, :, :], bi[:, :, :], bh[:, :, :], ALU.add).then_inc(bias_summed, 1)
            dve.tensor_scalar(bhn[:, :, :], bh[:, :, 2:3], 0.5, None, ALU.mult)
            dve.tensor_scalar(wqn[:, :], wqk[:, 0, :], -SCORE_SCALE, None, ALU.mult)
            dve.tensor_scalar(bqn[:, :], bqk[:, 0:1], -SCORE_SCALE, None, ALU.mult)
            dve.wait_ge(bias_summed, 1)
            dve.tensor_scalar(brz[:, :, :], brz[:, :, :], 0.5, None, ALU.mult).then_inc(w_ready, 1)
            dve.wait_ge(consts_ready, 4)
            dve.tensor_tensor(w0[:, 2, :], wu[:, 0, :], ident[:, :], ALU.add).then_inc(w_ready, 1)
            dve.wait_ge(fused_done, 1)
            dve.tensor_copy(w0[:, 0, :], bank[1][0][:, 0:FEATS]).then_inc(w_ready, 1)
            dve.tensor_copy(w0[:, 1, :], bank[1][0][:, FEATS:2 * FEATS]).then_inc(w_ready, 1)

            def stand_alone():
                dve.sem_inc(waited, 1)

            def seed_root(s, t, k):
                tick = t * TICKS + TICK_BASE[k] + ROOT_TICKS[k]
                dve.tensor_scalar(bits[s][:, :], ve[s][:, :].bitcast(I32), 1, None, ALU.logical_shift_right
                                  ).then_inc(norm_tick[s], 1)
                dve.tensor_scalar(vh[s][:, :], ve[s][:, :], -0.5, None, ALU.mult).then_inc(seeded[s], 1)
                dve.wait_ge(norm_tick[s], tick)
                dve.tensor_scalar(root[s][:, :].bitcast(I32), bits[s][:, :], -1.0, float(SEED), ALU.mult, ALU.add
                                  ).then_inc(seeded[s], 1)

            def norm(s, t, k, y_count):
                tick = t * TICKS + TICK_BASE[k]
                dve.wait_ge(y_ready[s], y_count) if y_count is not None else dve.wait_ge(combined[s], t * 9 + 9)
                for c in range(CHUNKS):
                    a = dve.bn_stats(stats[s][:, c, :], y[s][:, c, :])
                a.then_inc(norm_tick[s], 1)
                dve.wait_ge(norm_tick[s], tick + 1)
                stand_alone()
                for c in range(CHUNKS):
                    a = dve.bn_aggr(mv[s][:, c, :], stats[s][:, c, :])
                a.then_inc(norm_tick[s], 1)
                dve.wait_ge(norm_tick[s], tick + 2)
                dve.tensor_scalar(ve[s][:, :], mv[s][:, :, 1], LN_EPS, None, ALU.add).then_inc(norm_tick[s], 1)
                dve.wait_ge(norm_tick[s], tick + 3)
                seed_root(s, t, k)

            def apply(s, t, k, dst, ready):
                dve.wait_ge(newton[s], t * NEWTON_STEPS * ROOTS + NEWTON_STEPS * (k + 1))
                for c in range(CHUNKS):
                    a = dve.tensor_scalar(dst[:, c, :], y[s][:, c, :], mv[s][:, c, 0:1], root[s][:, c:c + 1],
                                          ALU.subtract, ALU.mult)
                a.then_inc(ready, 1)

            def norm1(s, t):
                W = FEATS + 1
                dve.wait_ge(messages_done[s], t + 1)
                first = chunks_of_sums = bank[s][3][:, 0:3 * W].rearrange("p (c f) -> p c f", c=3)
                last = bank[s][0][:, 0:W]
                dve.tensor_scalar(deg[s][:, 0:3], chunks_of_sums[:, :, FEATS], 1.0, None, ALU.max)
                dve.tensor_scalar(deg[s][:, 3:4], last[:, FEATS:W], 1.0, None, ALU.max).then_inc(combined[s], 1)
                dve.tensor_scalar(has[s][:, 0:3], first[:, :, FEATS], 0.0, None, ALU.is_gt)
                dve.tensor_scalar(has[s][:, 3:4], last[:, FEATS:W], 0.0, None, ALU.is_gt).then_inc(combined[s], 1)
                dve.wait_ge(combined[s], t * 9 + 1)
                dve.reciprocal(inv[s][:, :], deg[s][:, :]).then_inc(combined[s], 1)
                dve.wait_ge(combined[s], t * 9 + 3)
                dve.tensor_tensor(minv[s][:, :], inv[s][:, :], has[s][:, :], ALU.mult).then_inc(combined[s], 1)
                dve.tensor_tensor(y2[s][:, :, :], chunks(bank[s][1][:, :]), spread(has[s][:, :]), ALU.mult
                                  ).then_inc(combined[s], 1)
                dve.wait_ge(combined[s], t * 9 + 4)
                dve.tensor_tensor(y[s][:, 0:3, :], first[:, :, 0:FEATS], spread(minv[s][:, 0:3]), ALU.mult)
                dve.tensor_tensor(y[s][:, 3:4, :], last[:, 0:FEATS].unsqueeze(1), spread(minv[s][:, 3:4]), ALU.mult
                                  ).then_inc(combined[s], 1)
                dve.wait_ge(combined[s], t * 9 + 6)
                dve.tensor_tensor(y[s][:, :, :], y[s][:, :, :], y2[s][:, :, :], ALU.add).then_inc(combined[s], 1)
                dve.wait_ge(combined[s], t * 9 + 7)
                dve.tensor_tensor(y[s][:, :, :], y[s][:, :, :], chunks(bank[s][2][:, :]), ALU.add
                                  ).then_inc(combined[s], 2)
                norm(s, t, NORM1, None)

            def apply1(s, t):
                apply(s, t, NORM1, x1[s], x1_ready[s])

            def gates_sum(s, t, i):
                dve.wait_ge(hn_ready[s], t * LAYERS + i + 1)
                dve.wait_ge(reset_ready[s], t * LAYERS + i + 1)
                dve.scalar_tensor_tensor(cand[s][:, :], reset[s][:, :], 1.0, cand[s][:, :], ALU.add, ALU.mult
                                         ).then_inc(gated[s], 1)
                dve.wait_ge(gated[s], t * LAYERS + i + 1)
                dve.wait_ge(xn_done[s], t * LAYERS + i + 1)
                dve.tensor_tensor(cand[s][:, :], cand[s][:, :], bank[s][0][:, :], ALU.add).then_inc(cand_ready[s], 1)

            def update(s, t, i):
                dve.wait_ge(new_ready[s], t * LAYERS + i + 1)
                dve.tensor_tensor(diff[s][:, :], state[s][:, :], new[s][:, :], ALU.subtract).then_inc(diff_ready[s], 1)
                dve.wait_ge(keep_ready[s], t * LAYERS + i + 1)
                dve.wait_ge(diff_ready[s], t * 2 * LAYERS + 2 * i + 1)
                dve.scalar_tensor_tensor(diff[s][:, :], keep[s][:, :], 1.0, diff[s][:, :], ALU.add, ALU.mult
                                         ).then_inc(diff_ready[s], 1)
                dve.wait_ge(diff_ready[s], t * 2 * LAYERS + 2 * i + 2)
                dve.scalar_tensor_tensor(state[s][:, :], diff[s][:, :], 0.5, new[s][:, :], ALU.mult, ALU.add
                                         ).then_inc(state_ready[s], 1)

            def norm2(s, t):
                dve.wait_ge(state_turned[s], t * LAYERS + LAYERS)
                dve.tensor_tensor(y[s][:, :, :], chunks(bank[s][1][:, :]), spread(nmask[s][:, :]), ALU.mult
                                  ).then_inc(y_ready[s], 1)
                dve.wait_ge(y_ready[s], t * 5 + 2)
                dve.tensor_tensor(y[s][:, :, :], y[s][:, :, :], x1[s][:, :, :], ALU.add).then_inc(y_ready[s], 1)
                norm(s, t, NORM2, t * 5 + 3)

            def apply2(s, t):
                apply(s, t, NORM2, x2[s], x2_ready[s])

            def mask(s, t):
                dve.wait_ge(adj_loaded[s], t * DMA + DMA)
                dve.tensor_scalar(far[:, :, :], adj_s[s][:, :, :], 1.0, -MASK, ALU.subtract, ALU.mult
                                  ).then_inc(far_ready[s], 1)

            def qkv(s, t):
                for tensor, bias in ((0, bqn[:, 0:1]), (1, bqk[:, 1:2])):
                    dve.wait_ge(high_ready[s], t * 2 + tensor + 1)
                    dve.scalar_tensor_tensor(parts[:, LOW[tensor], :], bank[s][1 + tensor][:, :], bias,
                                             parts[:, HIGH[tensor], :].bitcast(F32), ALU.add, ALU.subtract
                                             ).then_inc(low_ready[s], 1)
                dve.wait_ge(qkv_done[s], t * 3 + 3)
                dve.tensor_tensor(vals[s][:, :, :], chunks(bank[s][3][:, :]), rows_of(bv_s[:, :]), ALU.add
                                  ).then_inc(vals_ready[s], 1)

            def degree(s, t):
                dve.wait_ge(deg3_ready[s], t + 1)
                dve.tensor_copy(ve[s][:, :], deg[s][:, :]).then_inc(norm_tick[s], 1)
                dve.wait_ge(norm_tick[s], t * TICKS + TICK_BASE[DEGREE] + 1)
                seed_root(s, t, DEGREE)

            def score(s, t, u):
                if u == 0:
                    dve.wait_ge(far_ready[s], t + 1)
                    dve.wait_ge(newton[s], t * NEWTON_STEPS * ROOTS + NEWTON_STEPS * (DEGREE + 1))
                    dve.tensor_copy(d3[s][:, :], root[s][:, :]).then_inc(d3_ready[s], 1)
                dve.wait_ge(scored[s], t * UNITS + u + 1)
                if u >= 2:
                    dve.wait_ge(prob_ready[s], t * UNITS + u - 1)
                stand_alone()
                dve.tensor_tensor_reduce(masked[u % 2][:, :], bank[s][1 + u % 2][:, :], far[:, u // HEADS, :],
                                         1.0, 3.0e38, ALU.add, ALU.min, low[s][:, u:u + 1]
                                         ).then_inc(masked_ready[s], 1)

            def mix(s, t, c):
                dve.wait_ge(mixed[s], t * CHUNKS + c + 1)
                dve.reciprocal(rsum[s][:, :], bank[s][0][:, P:2 * P]).then_inc(rsum_ready[s], 1)
                dve.wait_ge(rsum_ready[s], t * CHUNKS + c + 1)
                dve.tensor_tensor(ocol[s][:, c * P:c * P + P], bank[s][0][:, 0:P], rsum[s][:, :], ALU.mult
                                  ).then_inc(ocol_ready[s], 1)

            def merge(s, t):
                dve.wait_ge(merged[s], t + 1)
                dve.wait_ge(xb_ready[s], t * 2 + 1)
                dve.tensor_tensor(y[s][:, :, :], chunks(bank[s][1][:, :]), xb[s][:, :, :], ALU.add
                                  ).then_inc(y_ready[s], 1)
                norm(s, t, NORM3, t * 5 + 4)

            def apply3(s, t):
                apply(s, t, NORM3, x3[s], x3_ready[s])

            def support(s, t):
                dve.wait_ge(supported[s], t + 1)
                dve.wait_ge(d3_ready[s], t + 1)
                dve.tensor_tensor(supp[s][:, :, :], chunks(bank[s][2][:, :]), spread(d3[s][:, :]), ALU.mult
                                  ).then_inc(supp_ready[s], 1)

            def spread3(s, t):
                dve.wait_ge(spread_done[s], t + 1)
                dve.tensor_tensor(y[s][:, :, :], chunks(bank[s][3][:, :]), spread(d3[s][:, :]), ALU.mult
                                  ).then_inc(y_ready[s], 1)
                dve.wait_ge(y_ready[s], t * 5 + 5)
                dve.wait_ge(xb_ready[s], t * 2 + 2)
                dve.tensor_tensor(y[s][:, :, :], y[s][:, :, :], xb[s][:, :, :], ALU.add).then_inc(y_ready[s], 1)
                norm(s, t, NORM4, t * 5 + 6)

            def apply4(s, t):
                dve.wait_ge(stored[s], t * DMA + DMA)
                apply(s, t, NORM4, y4[s], y4_ready[s])

            run_phases(dve, {
                "norm1": norm1, "apply1": apply1, "gates_sum": gates_sum, "update": update, "norm2": norm2,
                "apply2": apply2, "mask": mask, "qkv": qkv, "degree": degree, "score": score, "mix": mix,
                "merge": merge, "apply3": apply3, "support": support, "spread": spread3, "apply4": apply4,
            })

        @block.gpsimd
        def _(pool):
            pool.memset(ident[:, :], 0.0).then_inc(ident_zeroed, 1)
            pool.memset(c15[:, :], 1.5)
            pool.wait_ge(ident_zeroed, 1)
            pool.affine_select(out=ident[:, :], in_=ident[:, :], compare_op=ALU.not_equal, fill=1.0, base=0,
                               pattern=[[-1, P]], channel_multiplier=1).then_inc(consts_ready, 1)
            pool.wait_ge(w_loaded, DMA * WEIGHT_LOADS)

            def newton_root(s, t, k):
                at = t * NEWTON_STEPS * ROOTS + NEWTON_STEPS * k
                pool.wait_ge(seeded[s], t * 2 * ROOTS + 2 * k + 2)
                for step in range(NEWTON_STEPS):
                    if step:
                        pool.wait_ge(newton[s], at + step)
                    out_, a, b, op = [
                        (sq[s], root[s], root[s], ALU.mult), (sq[s], sq[s], vh[s], ALU.mult),
                        (sq[s], sq[s], c15, ALU.add), (root[s], root[s], sq[s], ALU.mult)][step % 4]
                    pool.tensor_tensor(out_[:, :], a[:, :], b[:, :], op).then_inc(newton[s], 1)

            def diagonal(tile):
                blocks = tile[:, :, :].rearrange("p c (d m) -> p (c d) m", d=CHUNKS)
                return blocks[:, 0:CHUNKS * CHUNKS:CHUNKS + 1, :]

            def add_self(tile):
                return pool.tensor_tensor(diagonal(tile), diagonal(tile),
                                          ident[:, :].unsqueeze(1).broadcast_to([P, CHUNKS, P]), ALU.add)

            def norm1(s, t):
                newton_root(s, t, NORM1)

            def norm2(s, t):
                newton_root(s, t, NORM2)

            def degree(s, t):
                pool.wait_ge(aggregated[s], t * LAYERS + LAYERS)
                pool.wait_ge(far_ready[s], t + 1)
                add_self(adj_s[s]).then_inc(self_added[s], 1)
                newton_root(s, t, DEGREE)
                pool.wait_ge(x2_ready[s], t + 1)
                pool.wait_ge(y_ready[s], t * 5 + 1)
                pool.tensor_tensor(xb[s][:, :, :], x2[s][:, :, :], rows_of(bo_s[:, :]), ALU.add).then_inc(xb_ready[s], 1)
                pool.wait_ge(adjt_loaded[s], t * DMA + DMA)
                add_self(adjt_s[s]).then_inc(selft_added[s], 1)

            def merge(s, t):
                newton_root(s, t, NORM3)

            def apply3(s, t):
                pool.wait_ge(x3_ready[s], t + 1)
                pool.tensor_tensor(xb[s][:, :, :], x3[s][:, :, :], rows_of(b3_s[:, :]), ALU.add).then_inc(xb_ready[s], 1)

            def spread3(s, t):
                newton_root(s, t, NORM4)

            run_phases(pool, {"norm1": norm1, "norm2": norm2, "degree": degree, "merge": merge,
                              "apply3": apply3, "spread": spread3})


def kernel(x, adj, nodemask, L0_gnn_W_msg, L0_gnn_W_upd, L1_gnn_weight, L1_gnn_w_ih, L1_gnn_w_hh, L1_gnn_b_ih,
           L1_gnn_b_hh, L2_gnn_Wq, L2_gnn_bq, L2_gnn_Wk, L2_gnn_bk, L2_gnn_Wv, L2_gnn_bv, L2_gnn_Wo, L2_gnn_bo,
           L3_gnn_weight, L3_gnn_bias):
    import numpy as np
    import concourse.bacc as bacc
    from concourse.bass_utils import run_bass_kernel_spmd

    def turned(a):
        return np.swapaxes(np.asarray(a), -1, -2)

    def per_feature(a):
        return np.asarray(a).reshape(LAYERS, 3, FEATS).transpose(2, 0, 1)

    given = {
        "x_columns": turned(x), "adj": adj, "adj_t": turned(adj), "node_mask": turned(np.asarray(nodemask).reshape(GRAPHS, CHUNKS, P)),
        "w_msg_t": turned(L0_gnn_W_msg), "w_upd": L0_gnn_W_upd,
        "weight_t": turned(L1_gnn_weight), "w_ih_t": turned(L1_gnn_w_ih), "w_hh_t": turned(L1_gnn_w_hh),
        "b_ih": per_feature(L1_gnn_b_ih), "b_hh": per_feature(L1_gnn_b_hh),
        "wq": L2_gnn_Wq, "bq": np.asarray(L2_gnn_bq).reshape(FEATS, 1), "wk": L2_gnn_Wk, "bk": np.asarray(L2_gnn_bk).reshape(FEATS, 1), "wv": L2_gnn_Wv, "bv": L2_gnn_bv,
        "wo": L2_gnn_Wo, "bo": L2_gnn_bo, "w3": L3_gnn_weight, "b3": L3_gnn_bias,
    }
    nc = bacc.Bacc("TRN2", target_bir_lowering=False, num_devices=1)
    arrays, args = {}, {}
    for name, a in given.items():
        a = np.ascontiguousarray(a)
        arrays[f"in_{name}"] = a
        args[name] = nc.dram_tensor(f"in_{name}", a.shape, mybir.dt.from_np(a.dtype), kind="ExternalInput").ap()
    out = nc.dram_tensor("out", (GRAPHS, NODES, FEATS), F32, kind="ExternalOutput").ap()
    nc.disable_value_cache = True
    graph_layers(nc, **args, out=out)
    r = run_bass_kernel_spmd(nc, [arrays], core_ids=[0])
    return r.results[0]["out"]
```

```python
from collections import namedtuple
from contextlib import ExitStack

import concourse.bass as bass
from concourse import mybir

F32 = mybir.dt.float32
F32R = mybir.dt.float32r
I32 = mybir.dt.int32
ALU = mybir.AluOpType
ACT = mybir.ActivationFunctionType
AX = mybir.AxisListType

GRAPHS, NODES, FEATS = 16, 512, 128
P = 128
CHUNKS = NODES // P
LAYERS = 4
HEADS = 4
HEAD = FEATS // HEADS
UNITS = CHUNKS * HEADS
STRANDS = 2
TURNS = GRAPHS // STRANDS
LN_EPS = 1e-5
MASK = 1e9
SCORE_SCALE = float(HEAD) ** -0.5
DMA = 16

NORM2, DEGREE, NORM3, NORM4 = range(4)
ROOTS = 4
NEWTON_ROUNDS = 3
NEWTON_STEPS = 4 * NEWTON_ROUNDS
SEED = 0x5F3759DF
NORM_TICKS = 4
ROOT_TICKS = [NORM_TICKS, 2, NORM_TICKS, NORM_TICKS]
TICK_BASE = [sum(ROOT_TICKS[:k]) for k in range(ROOTS)]
TICKS = sum(ROOT_TICKS)
COMBINED = 9
SUMMED = 5
Root = namedtuple("Root", "y stats mv ve vh bits root sq tick seeded newton")
Q_LOW, Q_HIGH, K_HIGH, K_LOW = range(4)
PRODUCTS = [(Q_HIGH, K_HIGH), (Q_HIGH, K_LOW), (Q_LOW, K_HIGH), (Q_LOW, K_LOW)]
HIGH, LOW = (Q_HIGH, K_HIGH), (Q_LOW, K_LOW)
STACKS = len(PRODUCTS) * HEADS

FIRST = [("turn1",)]
for i in range(LAYERS):
    FIRST += [("aggregate", i, c) for c in range(CHUNKS)]
    FIRST += [("gates_state", i, gate) for gate in range(3)]
    FIRST += [("gates_sum", i, gate) for gate in range(3)]
    FIRST += [("update", i), ("turn_state", i)]
FIRST += [("norm2",), ("apply2",)]

LAYER0 = [("project",)] + [("message", c) for c in range(CHUNKS)] + [("receive", 0), ("receive", 1), ("norm1",), ("apply1",)]
SECOND = [("turn2",), ("mask",), ("qkv",), ("degree",), ("score", 0), ("score", 1)]
for u in range(UNITS):
    SECOND += [("weights", u)]
    if u + 2 < UNITS:
        SECOND += [("score", u + 2)]
    if u % HEADS == 0 and u:
        SECOND += [("sums", u // HEADS - 1)]
    if u % HEADS == 1 and u > HEADS:
        SECOND += [("mix", u // HEADS - 1)]
PROJECT, *MESSAGE, RECEIVE0, RECEIVE1, NORM1, APPLY1 = [("next", *step) for step in LAYER0]
SECOND += [("sums", CHUNKS - 1), ("mix", CHUNKS - 1), PROJECT, ("merge",), *MESSAGE, RECEIVE0, RECEIVE1,
           ("apply3",), NORM1, ("turn3",), ("support",), APPLY1]
SECOND += [("spread", c) for c in range(CHUNKS)] + [("apply4",)]

BEHIND = [0, 0, 0, 2, 1, 0, 0, 1, 0, 0, 0, 0, 0, 1, 1, 2, 1, 1, 2, 2, 2, 2, 0, 2, 2, 2, 3, 5, 1, 1, 3, 4, 2, 5, 0, 3, 1, 0, 1, 0, 0, 0, 0, 1, 1, 1, 0, 3, 0, 2, 1]


def phase_order():
    order, at = [], 0
    for step, n in zip(FIRST, BEHIND):
        order += [(0, step)] + [(1, x) for x in SECOND[at:at + n]]
        at += n
    return order + [(1, x) for x in SECOND[at:]]


PHASE = phase_order()


def walk(steps, first, second):
    for half, (name, *arg) in PHASE:
        if first is None and half == 0 or second is None and half == 1:
            continue
        s, t = (first, second)[half]
        if name == "next":
            if not more(t):
                continue
            t, name, arg = t + 1, arg[0], arg[1:]
        elif isinstance(t, int) and t < 0:
            continue
        if name in steps:
            steps[name](s, t, *arg)


def more(t):
    return not isinstance(t, int) or t + 1 < TURNS


def follows(t):
    return not isinstance(t, int) or t > 0


def run_phases(engine, steps):
    for name, *arg in LAYER0:
        if name in steps:
            steps[name](0, 0, *arg)
    if "fuse" in steps:
        steps["fuse"]()
    walk(steps, (0, 0), (1, -1))
    with engine.Fori(0, TURNS - 1) as t:
        walk(steps, (1, t), (0, t))
        walk(steps, (0, t + 1), (1, t))
    walk(steps, (1, TURNS - 1), (0, TURNS - 1))
    walk(steps, None, (1, TURNS - 1))


def graph_layers(nc, x_columns, adj, adj_t, node_mask, w_msg_t, w_upd, weight_t, w_ih_t, w_hh_t, b_ih, b_hh,
                 wq, bq, wk, bk, wv, bv, wo, bo, w3, b3, out):
    ctx = ExitStack()
    with ctx:
        def sb(name, shape, dt=F32):
            return ctx.enter_context(nc.sbuf_tensor(name, shape, dt))

        def pair(name, shape, dt=F32):
            return [sb(f"{name}{s}", shape, dt) for s in range(STRANDS)]

        def sem(name):
            return ctx.enter_context(nc.semaphore(name))

        def sems(name):
            return [sem(f"{name}{s}") for s in range(STRANDS)]

        ident = sb("ident", [P, P])
        c15 = sb("c15", [P, CHUNKS])
        wmt = sb("wmt", [P, 2 * FEATS])
        wu = sb("wu", [P, 2, FEATS])
        w0 = sb("w0", [P, 3, FEATS])
        wt = sb("wt", [P, LAYERS, FEATS])
        wih = sb("wih", [P, LAYERS, 3 * FEATS])
        wwi = sb("wwi", [P, LAYERS, 3 * FEATS])
        whh = sb("whh", [P, LAYERS, 3 * FEATS])
        bi = sb("bi", [P, LAYERS, 3])
        bh = sb("bh", [P, LAYERS, 3])
        brz = sb("brz", [P, LAYERS, 3])
        bhn = sb("bhn", [P, LAYERS, 1])
        wqk = sb("wqk", [P, 2, FEATS])
        bqk = sb("bqk", [P, 2])
        wqn = sb("wqn", [P, FEATS])
        bqn = sb("bqn", [P, 1])
        wv_s = sb("wv_s", [P, FEATS])
        wo_s = sb("wo_s", [P, FEATS])
        w3_s = sb("w3_s", [P, FEATS])
        bv_s = sb("bv_s", [P, FEATS])
        bo_s = sb("bo_s", [P, FEATS])
        b3_s = sb("b3_s", [P, FEATS])

        adj_s = pair("adj_s", [P, CHUNKS, NODES])
        adjt_s = pair("adjt_s", [P, CHUNKS, NODES])
        xcol = pair("xcol", [P, NODES])
        nmask = pair("nmask", [P, CHUNKS])
        mine = sb("mine", [P, CHUNKS, FEATS])
        sent = pair("sent", [P, CHUNKS, FEATS + 1])
        deg = pair("deg", [P, CHUNKS])
        has = pair("has", [P, CHUNKS])
        inv = pair("inv", [P, CHUNKS])
        minv = pair("minv", [P, CHUNKS])
        deg3 = pair("deg3", [P, CHUNKS])
        d3 = pair("d3", [P, CHUNKS])
        x1 = pair("x1", [P, CHUNKS, FEATS])
        state = pair("state", [P, NODES])
        state_rows = pair("state_rows", [P, CHUNKS, FEATS])
        aggr = pair("aggr", [P, NODES])
        cand = pair("cand", [P, NODES])
        reset = pair("reset", [P, NODES])
        keep = pair("keep", [P, NODES])
        new = pair("new", [P, NODES])
        diff = pair("diff", [P, NODES])
        x2 = pair("x2", [P, CHUNKS, FEATS])
        x3 = pair("x3", [P, CHUNKS, FEATS])
        xb = pair("xb", [P, CHUNKS, FEATS])
        xturn = pair("xturn", [P, NODES])
        vals = pair("vals", [P, CHUNKS, FEATS])
        low = pair("low", [P, UNITS])
        esum = pair("esum", [P, UNITS])
        einv = pair("einv", [P, HEADS])
        rwide = pair("rwide", [P, HEADS, HEAD])
        rsumt = pair("rsumt", [P, P])
        ocol = pair("ocol", [P, NODES])
        y4 = pair("y4", [P, CHUNKS, FEATS])

        def root_of(name):
            tiles = [pair(name + "_y", [P, CHUNKS, FEATS]), pair(name + "_stats", [P, CHUNKS, 6]),
                     pair(name + "_mv", [P, CHUNKS, 2]), pair(name + "_ve", [P, CHUNKS]),
                     pair(name + "_vh", [P, CHUNKS]), pair(name + "_bits", [P, CHUNKS], I32),
                     pair(name + "_root", [P, CHUNKS]), pair(name + "_sq", [P, CHUNKS])]
            chains = [sems(name + "_tick"), sems(name + "_seeded"), sems(name + "_newton")]
            return [Root(*parts_of) for parts_of in zip(*tiles, *chains)]

        first_root = root_of("first")
        later_root = root_of("later")

        supp = sb("supp", [P, CHUNKS, FEATS])
        far = sb("far", [P, CHUNKS, NODES])
        parts = sb("parts", [P, 4, NODES], F32R)
        stack = sb("stack", [P, 2, HEADS, NODES], F32R)
        masked = [sb(f"masked{b}", [P, NODES]) for b in range(2)]
        prob = [sb(f"prob{b}", [P, NODES]) for b in range(2)]
        prob_t = [sb(f"prob_t{b}", [P, CHUNKS, HEADS, P]) for b in range(2)]

        bank = [[ctx.enter_context(nc.psum_tensor(f"bank{s}{b}", [P, NODES], F32)) for b in range(4)]
                for s in range(STRANDS)]

        def chunks(ap):
            return ap.rearrange("p (c f) -> p c f", c=CHUNKS)

        def spread(ap, n=FEATS):
            return ap.unsqueeze(2).broadcast_to([P, ap.shape[1], n])

        def rows_of(ap):
            return ap.unsqueeze(1).broadcast_to([P, CHUNKS, FEATS])

        w0_loaded = sem("w0_loaded")
        w_loaded = sem("w_loaded")
        bias_summed = sem("bias_summed")
        bias_ready = sem("bias_ready")
        waited = sem("waited")
        ident_zeroed = sem("ident_zeroed")
        consts_ready = sem("consts_ready")
        fused0_done = sem("fused0_done")
        w0_ready = sem("w0_ready")
        fused_done = sem("fused_done")
        w_ready = sem("w_ready")
        x_loaded = sems("x_loaded")
        adj_loaded = sems("adj_loaded")
        adjt_loaded = sems("adjt_loaded")
        projected = sems("projected")
        sent_ready = sems("sent_ready")
        messages_done = sems("messages_done")
        received = sems("received")
        combined = sems("combined")
        x1_ready = sems("x1_ready")
        x1_turned = sems("x1_turned")
        state0_ready = sems("state0_ready")
        aggregated = sems("aggregated")
        aggr_ready = sems("aggr_ready")
        hn_done = sems("hn_done")
        r_done = sems("r_done")
        xn_done = sems("xn_done")
        z_done = sems("z_done")
        hn_ready = sems("hn_ready")
        reset_ready = sems("reset_ready")
        gated = sems("gated")
        cand_ready = sems("cand_ready")
        new_ready = sems("new_ready")
        keep_ready = sems("keep_ready")
        diff_ready = sems("diff_ready")
        state_ready = sems("state_ready")
        state_turned = sems("state_turned")
        rows_ready = sems("rows_ready")
        y_ready = sems("y_ready")
        x2_ready = sems("x2_ready")
        x2_turned = sems("x2_turned")
        x2col_ready = sems("x2col_ready")
        qkv_done = sems("qkv_done")
        high_ready = sems("high_ready")
        low_ready = sems("low_ready")
        vals_ready = sems("vals_ready")
        stacked = sems("stacked")
        far_ready = sems("far_ready")
        self_added = sems("self_added")
        selft_added = sems("selft_added")
        deg3_ready = sems("deg3_ready")
        d3_ready = sems("d3_ready")
        scored = sems("scored")
        masked_ready = sems("masked_ready")
        prob_ready = sems("prob_ready")
        prob_turned = sems("prob_turned")
        probt_ready = sems("probt_ready")
        mixed = sems("mixed")
        rsum_ready = sems("rsum_ready")
        rsumt_ready = sems("rsumt_ready")
        ocol_ready = sems("ocol_ready")
        xb_ready = sems("xb_ready")
        merged = sems("merged")
        x3_ready = sems("x3_ready")
        x3_turned = sems("x3_turned")
        x3col_ready = sems("x3col_ready")
        supported = sems("supported")
        supp_ready = sems("supp_ready")
        spread_done = sems("spread_done")
        y4_ready = sems("y4_ready")
        stored = sems("stored")

        WEIGHT_LOADS = 15
        block = ctx.enter_context(nc.Block())

        @block.sync
        def _(sp):
            def load_x(s, t):
                sp.dma_start(xcol[s][:, :], x_columns[t * STRANDS + s]).then_inc(x_loaded[s], DMA)
                sp.dma_start(nmask[s][:, :], node_mask[t * STRANDS + s]
                             ).then_inc(x_loaded[s], DMA)

            def load_adj(s, t):
                sp.dma_start(adj_s[s][:, :, :], adj[t * STRANDS + s].rearrange("(c p) m -> p c m", p=P)
                             ).then_inc(adj_loaded[s], DMA)

            def load_adjt(s, t):
                sp.dma_start(adjt_s[s][:, :, :], adj_t[t * STRANDS + s].rearrange("(c p) m -> p c m", p=P)
                             ).then_inc(adjt_loaded[s], DMA)

            load_x(0, 0)
            for tile, src in (
                (wmt[:, :], w_msg_t), (wu[:, :, :], w_upd.rearrange("(h k) n -> k h n", h=2)),
            ):
                sp.dma_start(tile, src).then_inc(w0_loaded, DMA)
            load_adj(0, 0)
            for tile, src in (
                (wt[:, :, :], weight_t.rearrange("l d c -> d l c")), (wih[:, :, :], w_ih_t.rearrange("l d g -> d l g")),
                (whh[:, :, :], w_hh_t.rearrange("l d g -> d l g")),
                (bi[:, :, :], b_ih), (bh[:, :, :], b_hh),
                (wqk[:, 0, :], wq), (wqk[:, 1, :], wk),
                (bqk[:, 0:1], bq), (bqk[:, 1:2], bk),
                (wv_s[:, :], wv), (wo_s[:, :], wo), (w3_s[:, :], w3),
                (bv_s[:, :], bv.partition_broadcast(P)), (bo_s[:, :], bo.partition_broadcast(P)),
                (b3_s[:, :], b3.partition_broadcast(P)),
            ):
                sp.dma_start(tile, src).then_inc(w_loaded, DMA)
            load_adjt(0, 0)
            load_x(1, 0)
            load_adj(1, 0)
            load_adjt(1, 0)

            def qkv(s, t):
                sp.wait_ge(high_ready[s], t * 2 + 2)
                sp.wait_ge(low_ready[s], t * 2 + 2)
                for h in range(HEADS):
                    rows = slice(HEAD * h, HEAD * h + HEAD)
                    for quadrant, (q, k) in enumerate(PRODUCTS):
                        sp.dma_start(stack[HEAD * quadrant:HEAD * quadrant + HEAD, :, h, :].bitcast(F32),
                                     parts[rows, q:k + 1:k - q, :].bitcast(F32)).then_inc(stacked[s], DMA)

            def degree(s, t):
                if more(t):
                    sp.wait_ge(x2_ready[s], t + 1)
                    load_x(s, t + 1)
                    sp.wait_ge(deg3_ready[s], t + 1)
                    load_adj(s, t + 1)

            def apply4(s, t):
                if more(t):
                    sp.wait_ge(spread_done[s], t + 1)
                    load_adjt(s, t + 1)
                sp.wait_ge(y4_ready[s], t + 1)
                sp.dma_start(out[t * STRANDS + s].rearrange("(c p) f -> p c f", p=P), y4[s][:, :, :]
                             ).then_inc(stored[s], DMA)

            run_phases(sp, {"qkv": qkv, "degree": degree, "apply4": apply4})
            for s in range(STRANDS):
                sp.wait_ge(stored[s], DMA * TURNS + DMA)

        @block.tensor
        def _(pe):
            pe.wait_ge(w0_loaded, 2 * DMA)
            for h in range(2):
                mm = pe.matmul(bank[1][0][:, h * FEATS:h * FEATS + FEATS], wmt[:, h * FEATS:h * FEATS + FEATS],
                               wu[:, 1, :], start=(h == 0), stop=(h == 1), skip_group_check=True)
            mm.then_inc(fused0_done, 1)
            pe.wait_ge(consts_ready, 3)
            pe.wait_ge(w0_ready, 3)

            def fuse():
                pe.wait_ge(w_loaded, DMA * WEIGHT_LOADS)
                for i in range(LAYERS):
                    last = pe.matmul(bank[1][i][:, 0:3 * FEATS], wt[:, i, :], wih[:, i, :], start=True, stop=True)
                last.then_inc(fused_done, 1)
                pe.wait_ge(w_ready, LAYERS)
                pe.wait_ge(bias_ready, 4)

            def by_rows(dst, columns, w):
                for c in range(CHUNKS):
                    mm = pe.matmul(dst[:, c * P:c * P + P], columns[:, c * P:c * P + P], w,
                                   start=(c == 0), stop=(c == CHUNKS - 1), skip_group_check=True)
                return mm

            def project(s, t):
                pe.wait_ge(x_loaded[s], t * 2 * DMA + 2 * DMA)
                if follows(t):
                    pe.wait_ge(masked_ready[s], t * UNITS)
                by_rows(bank[s][1], xcol[s], w0[:, 0, :]).then_inc(projected[s], 1)

            def message(s, t, r):
                if r == 0:
                    pe.wait_ge(sent_ready[s], t + 1)
                    pe.wait_ge(adj_loaded[s], t * DMA + DMA)
                    if follows(t):
                        pe.wait_ge(probt_ready[s], t * UNITS)
                W = FEATS + 1
                dst = bank[s][3][:, r * W:r * W + W] if r < 3 else bank[s][1][:, 0:W]
                for c in range(CHUNKS):
                    mm = pe.matmul(dst, adj_s[s][:, c, r * P:r * P + P], sent[s][:, c, :],
                                   start=(c == 0), stop=(c == CHUNKS - 1), skip_group_check=True)
                if r == CHUNKS - 1:
                    mm.then_inc(messages_done[s], 1)

            def receive(s, t, part):
                if follows(t) and part == 0:
                    pe.wait_ge(ocol_ready[s], t * CHUNKS)
                if follows(t) and part == 1:
                    pe.wait_ge(y_ready[s], t * SUMMED - 1)
                by_rows(bank[s][2 * part], xcol[s], w0[:, 1 + part, :]).then_inc(received[s], 1)

            def turn(dst, rows):
                for c in range(CHUNKS):
                    mm = pe.transpose(dst[:, c * P:c * P + P], rows(c), ident[:, :])
                return mm

            def turn1(s, t):
                pe.wait_ge(x1_ready[s], t + 1)
                pe.wait_ge(y_ready[s], t * SUMMED + 1)
                turn(bank[s][1], lambda c: x1[s][:, c, :]).then_inc(x1_turned[s], 1)

            def aggregate(s, t, i, c):
                if c == 0 and i == 0:
                    pe.wait_ge(x1_ready[s], t + 1)
                elif c == 0:
                    pe.wait_ge(rows_ready[s], t * (LAYERS - 1) + i)
                rows = x1[s] if i == 0 else state_rows[s]
                mm = pe.matmul(bank[s][0][:, :], rows[:, c, :], adj_s[s][:, c, :],
                               start=(c == 0), stop=(c == CHUNKS - 1))
                if c == CHUNKS - 1:
                    mm.then_inc(aggregated[s], 1)

            R, Z, N = (slice(g * FEATS, g * FEATS + FEATS) for g in range(3))

            def gates_state(s, t, i, gate):
                if i == 0 and gate == 0:
                    pe.wait_ge(state0_ready[s], t + 1)
                if gate == 0:
                    pe.matmul(bank[s][3][:, :], whh[:, i, N], state[s][:, :], start=True, stop=True
                              ).then_inc(hn_done[s], 1)
                else:
                    pe.matmul(bank[s][gate][:, :], whh[:, i, (R, Z)[gate - 1]], state[s][:, :],
                              start=True, stop=False)

            def gates_sum(s, t, i, gate):
                if gate == 0:
                    pe.wait_ge(aggr_ready[s], t * LAYERS + i + 1)
                    pe.matmul(bank[s][1][:, :], wwi[:, i, R], aggr[s][:, :], start=False, stop=True
                              ).then_inc(r_done[s], 1)
                elif gate == 1:
                    pe.matmul(bank[s][0][:, :], wwi[:, i, N], aggr[s][:, :], start=True, stop=True
                              ).then_inc(xn_done[s], 1)
                else:
                    pe.matmul(bank[s][2][:, :], wwi[:, i, Z], aggr[s][:, :], start=False, stop=True
                              ).then_inc(z_done[s], 1)

            def turn_state(s, t, i):
                pe.wait_ge(state_ready[s], t * LAYERS + i + 1)
                turn(bank[s][1], lambda c: state[s][:, c * P:c * P + P]).then_inc(state_turned[s], 1)

            def turn2(s, t):
                pe.wait_ge(x2_ready[s], t + 1)
                turn(bank[s][0], lambda c: x2[s][:, c, :]).then_inc(x2_turned[s], 1)

            def qkv(s, t):
                pe.wait_ge(x2col_ready[s], t + 1)
                pe.matmul(bank[s][1][:, :], wqn[:, :], xturn[s][:, :], start=True, stop=True
                          ).then_inc(qkv_done[s], 1)
                pe.matmul(bank[s][2][:, :], wqk[:, 1, :], xturn[s][:, :], start=True, stop=True
                          ).then_inc(qkv_done[s], 1)
                by_rows(bank[s][3], xturn[s], wv_s[:, :]).then_inc(qkv_done[s], 1)

            def score(s, t, u):
                c, h = u // HEADS, u % HEADS
                if u == 0:
                    pe.wait_ge(stacked[s], t * DMA * STACKS + DMA * STACKS)
                if u >= 2:
                    pe.wait_ge(masked_ready[s], t * UNITS + u - 1)
                pe.matmul(bank[s][1 + u % 2][:, :], stack[:, 0, h, c * P:c * P + P], stack[:, 1, h, :],
                          start=True, stop=True).then_inc(scored[s], 1)

            def weights(s, t, u):
                if u == 0:
                    pe.wait_ge(vals_ready[s], t + 1)
                else:
                    pe.wait_ge(probt_ready[s], t * UNITS + u)
                pe.wait_ge(prob_ready[s], t * UNITS + u + 1)
                turn(bank[s][3], lambda m: prob[u % 2][:, m * P:m * P + P]).then_inc(prob_turned[s], 1)

            def mix(s, t, c):
                pe.wait_ge(probt_ready[s], t * UNITS + HEADS * c + HEADS)
                if c:
                    pe.wait_ge(ocol_ready[s], t * CHUNKS + c)
                for m in range(CHUNKS):
                    for h in range(HEADS):
                        rows = slice(HEAD * h, HEAD * h + HEAD)
                        pe.matmul(bank[s][0][rows, 0:P], vals[s][:, m, rows], prob_t[c % 2][:, m, h, :],
                                  start=(m == 0), stop=(m == CHUNKS - 1), skip_group_check=True)
                pe.wait_ge(rsum_ready[s], t * 2 * CHUNKS + 2 * c + 2)
                pe.transpose(bank[s][0][:, P:2 * P], rwide[s][:, :, :].rearrange("p h d -> p (h d)"), ident[:, :]
                             ).then_inc(mixed[s], 1)

            def merge(s, t):
                pe.wait_ge(ocol_ready[s], t * CHUNKS + CHUNKS)
                pe.wait_ge(masked_ready[s], t * UNITS + UNITS)
                by_rows(bank[s][2], ocol[s], wo_s[:, :]).then_inc(merged[s], 1)

            def turn3(s, t):
                pe.wait_ge(x3_ready[s], t + 1)
                if more(t):
                    pe.wait_ge(combined[s], t * COMBINED + 2 * COMBINED)
                turn(bank[s][1], lambda c: x3[s][:, c, :]).then_inc(x3_turned[s], 1)

            def support(s, t):
                pe.wait_ge(x3col_ready[s], t + 1)
                by_rows(bank[s][0], xturn[s], w3_s[:, :]).then_inc(supported[s], 1)

            def spread3(s, t, n):
                if n == 0:
                    pe.wait_ge(selft_added[s], t + 1)
                    pe.wait_ge(supp_ready[s], t + 1)
                for m in range(CHUNKS):
                    mm = pe.matmul(bank[s][3][:, n * P:n * P + P], adjt_s[s][:, m, n * P:n * P + P],
                                   supp[:, m, :], start=(m == 0), stop=(m == CHUNKS - 1),
                                   skip_group_check=True)
                if n == CHUNKS - 1:
                    mm.then_inc(spread_done[s], 1)

            run_phases(pe, {
                "fuse": fuse,
                "project": project, "message": message, "receive": receive, "turn1": turn1,
                "aggregate": aggregate, "gates_state": gates_state, "gates_sum": gates_sum,
                "turn_state": turn_state, "turn2": turn2, "qkv": qkv, "score": score, "weights": weights,
                "mix": mix, "merge": merge, "turn3": turn3, "support": support, "spread": spread3,
            })

        @block.scalar
        def _(act):
            def fuse():
                act.wait_ge(fused_done, 1)
                for i in range(LAYERS):
                    act.copy(wwi[:, i, :], bank[1][i][:, 0:3 * FEATS]).then_inc(w_ready, 1)
                act.wait_ge(bias_ready, 4)

            def project(s, t):
                act.wait_ge(projected[s], t + 1)
                act.copy(sent[s][:, :, 0:FEATS], chunks(bank[s][1][:, :])).then_inc(sent_ready[s], 1)

            def turn1(s, t):
                act.wait_ge(x1_turned[s], t + 1)
                act.copy(state[s][:, :], bank[s][1][:, :]).then_inc(state0_ready[s], 1)

            def aggregate(s, t, i, c):
                if c < CHUNKS - 1:
                    return
                act.wait_ge(aggregated[s], t * LAYERS + i + 1)
                act.copy(aggr[s][:, :], bank[s][0][:, :]).then_inc(aggr_ready[s], 1)

            def gates_state(s, t, i, gate):
                if gate:
                    return
                act.wait_ge(hn_done[s], t * LAYERS + i + 1)
                act.activation(cand[s][:, :], bank[s][3][:, :], ACT.Identity, bias=bhn[:, i, :], scale=0.5
                               ).then_inc(hn_ready[s], 1)

            def gates_sum(s, t, i, gate):
                if gate:
                    return
                act.wait_ge(r_done[s], t * LAYERS + i + 1)
                act.activation(reset[s][:, :], bank[s][1][:, :], ACT.Tanh, bias=brz[:, i, 0:1], scale=0.5
                               ).then_inc(reset_ready[s], 1)

            def update(s, t, i):
                act.wait_ge(cand_ready[s], t * LAYERS + i + 1)
                act.activation(new[s][:, :], cand[s][:, :], ACT.Tanh, bias=bi[:, i, 2:3], scale=1.0
                               ).then_inc(new_ready[s], 1)
                act.wait_ge(z_done[s], t * LAYERS + i + 1)
                act.activation(keep[s][:, :], bank[s][2][:, :], ACT.Tanh, bias=brz[:, i, 1:2], scale=0.5
                               ).then_inc(keep_ready[s], 1)

            def turn_state(s, t, i):
                if i < LAYERS - 1:
                    act.wait_ge(state_turned[s], t * LAYERS + i + 1)
                    act.copy(state_rows[s][:, :, :], chunks(bank[s][1][:, :])).then_inc(rows_ready[s], 1)

            def turn2(s, t):
                act.wait_ge(x2_turned[s], t + 1)
                act.copy(xturn[s][:, :], bank[s][0][:, :]).then_inc(x2col_ready[s], 1)

            def qkv(s, t):
                for tensor, bias in ((0, bqn[:, 0:1]), (1, bqk[:, 1:2])):
                    act.wait_ge(qkv_done[s], t * 3 + tensor + 1)
                    act.activation(parts[:, HIGH[tensor], :], bank[s][1 + tensor][:, :], ACT.Identity,
                                   bias=bias, scale=1.0).then_inc(high_ready[s], 1)

            def degree(s, t):
                act.wait_ge(self_added[s], t + 1)
                for c in range(CHUNKS):
                    a = act.activation(adj_s[s][:, c, :], adj_s[s][:, c, :], ACT.Abs,
                                       accum_out=deg3[s][:, c:c + 1])
                a.then_inc(deg3_ready[s], 1)

            def score(s, t, u):
                act.wait_ge(masked_ready[s], t * UNITS + u + 1)
                if u >= 2:
                    act.wait_ge(prob_turned[s], t * UNITS + u - 1)
                act.activation(prob[u % 2][:, :], masked[u % 2][:, :], ACT.Exp, bias=low[s][:, u:u + 1],
                               scale=-1.0, accum_out=esum[s][:, u:u + 1]).then_inc(prob_ready[s], 1)

            def weights(s, t, u):
                c, h = u // HEADS, u % HEADS
                act.wait_ge(prob_turned[s], t * UNITS + u + 1)
                if c >= 2:
                    act.wait_ge(mixed[s], t * CHUNKS + c - 1)
                act.copy(prob_t[c % 2][:, :, h, :], chunks(bank[s][3][:, :])).then_inc(probt_ready[s], 1)

            def mix(s, t, c):
                act.wait_ge(mixed[s], t * CHUNKS + c + 1)
                act.copy(rsumt[s][:, :], bank[s][0][:, P:2 * P]).then_inc(rsumt_ready[s], 1)

            def turn3(s, t):
                act.wait_ge(x3_turned[s], t + 1)
                act.copy(xturn[s][:, :], bank[s][1][:, :]).then_inc(x3col_ready[s], 1)

            run_phases(act, {
                "fuse": fuse,
                "project": project, "turn1": turn1, "aggregate": aggregate, "gates_state": gates_state,
                "gates_sum": gates_sum, "update": update, "turn_state": turn_state, "turn2": turn2, "qkv": qkv,
                "degree": degree, "score": score, "weights": weights, "mix": mix, "turn3": turn3,
            })

        @block.vector
        def _(dve):
            for s in range(STRANDS):
                dve.sem_inc(y_ready[s], 1)
                dve.sem_inc(stored[s], DMA)
                dve.memset(sent[s][:, :, FEATS:FEATS + 1], 1.0).then_inc(consts_ready, 1)
            dve.wait_ge(w0_loaded, 2 * DMA)
            dve.wait_ge(consts_ready, 3)
            dve.tensor_tensor(w0[:, 2, :], wu[:, 0, :], ident[:, :], ALU.add).then_inc(w0_ready, 1)
            dve.wait_ge(fused0_done, 1)
            dve.tensor_copy(w0[:, 0, :], bank[1][0][:, 0:FEATS]).then_inc(w0_ready, 1)
            dve.tensor_copy(w0[:, 1, :], bank[1][0][:, FEATS:2 * FEATS]).then_inc(w0_ready, 1)
            dve.wait_ge(w_loaded, DMA * WEIGHT_LOADS)
            dve.tensor_tensor(brz[:, :, :], bi[:, :, :], bh[:, :, :], ALU.add).then_inc(bias_summed, 1)
            dve.tensor_scalar(bhn[:, :, :], bh[:, :, 2:3], 0.5, None, ALU.mult).then_inc(bias_ready, 1)
            dve.tensor_scalar(wqn[:, :], wqk[:, 0, :], -SCORE_SCALE, None, ALU.mult).then_inc(bias_ready, 1)
            dve.tensor_scalar(bqn[:, :], bqk[:, 0:1], -SCORE_SCALE, None, ALU.mult).then_inc(bias_ready, 1)
            dve.wait_ge(bias_summed, 1)
            dve.tensor_scalar(brz[:, :, :], brz[:, :, :], 0.5, None, ALU.mult).then_inc(bias_ready, 1)

            def stand_alone():
                dve.sem_inc(waited, 1)

            def seed_root(r, tick):
                dve.tensor_scalar(r.bits[:, :], r.ve[:, :].bitcast(I32), 1, None, ALU.logical_shift_right
                                  ).then_inc(r.tick, 1)
                dve.tensor_scalar(r.vh[:, :], r.ve[:, :], -0.5, None, ALU.mult).then_inc(r.seeded, 1)
                dve.wait_ge(r.tick, tick + 1)
                dve.tensor_scalar(r.root[:, :].bitcast(I32), r.bits[:, :], -1.0, float(SEED), ALU.mult, ALU.add
                                  ).then_inc(r.seeded, 1)

            def norm(r, tick):
                for c in range(CHUNKS):
                    a = dve.bn_stats(r.stats[:, c, :], r.y[:, c, :])
                a.then_inc(r.tick, 1)
                dve.wait_ge(r.tick, tick + 1)
                stand_alone()
                for c in range(CHUNKS):
                    a = dve.bn_aggr(r.mv[:, c, :], r.stats[:, c, :])
                a.then_inc(r.tick, 1)
                dve.wait_ge(r.tick, tick + 2)
                dve.tensor_scalar(r.ve[:, :], r.mv[:, :, 1], LN_EPS, None, ALU.add).then_inc(r.tick, 1)
                dve.wait_ge(r.tick, tick + 3)
                seed_root(r, tick + 3)

            def later_norm(s, t, k, summed):
                dve.wait_ge(y_ready[s], t * SUMMED + summed)
                norm(later_root[s], t * TICKS + TICK_BASE[k])

            def apply(r, rooted, dst, ready):
                dve.wait_ge(r.newton, rooted)
                for c in range(CHUNKS):
                    a = dve.tensor_scalar(dst[:, c, :], r.y[:, c, :], r.mv[:, c, 0:1], r.root[:, c:c + 1],
                                          ALU.subtract, ALU.mult)
                a.then_inc(ready, 1)

            def rooted(t, k):
                return t * NEWTON_STEPS * ROOTS + NEWTON_STEPS * (k + 1)

            def norm1(s, t):
                W = FEATS + 1
                at = t * COMBINED
                total = first_root[s].y
                dve.wait_ge(messages_done[s], t + 1)
                sums = bank[s][3][:, 0:3 * W].rearrange("p (c f) -> p c f", c=3)
                last = bank[s][1][:, 0:W]
                dve.tensor_scalar(deg[s][:, 0:3], sums[:, :, FEATS], 1.0, None, ALU.max)
                dve.tensor_scalar(deg[s][:, 3:4], last[:, FEATS:W], 1.0, None, ALU.max).then_inc(combined[s], 1)
                dve.tensor_scalar(has[s][:, 0:3], sums[:, :, FEATS], 0.0, None, ALU.is_gt)
                dve.tensor_scalar(has[s][:, 3:4], last[:, FEATS:W], 0.0, None, ALU.is_gt).then_inc(combined[s], 1)
                dve.wait_ge(combined[s], at + 1)
                dve.reciprocal(inv[s][:, :], deg[s][:, :]).then_inc(combined[s], 1)
                dve.wait_ge(combined[s], at + 3)
                dve.tensor_tensor(minv[s][:, :], inv[s][:, :], has[s][:, :], ALU.mult).then_inc(combined[s], 1)
                dve.wait_ge(received[s], t * 2 + 1)
                dve.tensor_tensor(mine[:, :, :], chunks(bank[s][0][:, :]), spread(has[s][:, :]), ALU.mult
                                  ).then_inc(combined[s], 1)
                dve.wait_ge(combined[s], at + 4)
                dve.tensor_tensor(total[:, 0:3, :], sums[:, :, 0:FEATS], spread(minv[s][:, 0:3]), ALU.mult)
                dve.tensor_tensor(total[:, 3:4, :], last[:, 0:FEATS].unsqueeze(1), spread(minv[s][:, 3:4]), ALU.mult
                                  ).then_inc(combined[s], 1)
                dve.wait_ge(combined[s], at + 6)
                dve.tensor_tensor(total[:, :, :], total[:, :, :], mine[:, :, :], ALU.add).then_inc(combined[s], 1)
                dve.wait_ge(combined[s], at + 7)
                dve.wait_ge(received[s], t * 2 + 2)
                dve.tensor_tensor(total[:, :, :], total[:, :, :], chunks(bank[s][2][:, :]), ALU.add
                                  ).then_inc(combined[s], 2)
                dve.wait_ge(combined[s], at + 9)
                norm(first_root[s], t * NORM_TICKS)

            def apply1(s, t):
                apply(first_root[s], t * NEWTON_STEPS + NEWTON_STEPS, x1[s], x1_ready[s])

            def gates_sum(s, t, i, gate):
                if gate != 1:
                    return
                dve.wait_ge(hn_ready[s], t * LAYERS + i + 1)
                dve.wait_ge(reset_ready[s], t * LAYERS + i + 1)
                dve.scalar_tensor_tensor(cand[s][:, :], reset[s][:, :], 1.0, cand[s][:, :], ALU.add, ALU.mult
                                         ).then_inc(gated[s], 1)
                dve.wait_ge(gated[s], t * LAYERS + i + 1)
                dve.wait_ge(xn_done[s], t * LAYERS + i + 1)
                dve.tensor_tensor(cand[s][:, :], cand[s][:, :], bank[s][0][:, :], ALU.add).then_inc(cand_ready[s], 1)

            def update(s, t, i):
                dve.wait_ge(new_ready[s], t * LAYERS + i + 1)
                dve.tensor_tensor(diff[s][:, :], state[s][:, :], new[s][:, :], ALU.subtract).then_inc(diff_ready[s], 1)
                dve.wait_ge(keep_ready[s], t * LAYERS + i + 1)
                dve.wait_ge(diff_ready[s], t * 2 * LAYERS + 2 * i + 1)
                dve.scalar_tensor_tensor(diff[s][:, :], keep[s][:, :], 1.0, diff[s][:, :], ALU.add, ALU.mult
                                         ).then_inc(diff_ready[s], 1)
                dve.wait_ge(diff_ready[s], t * 2 * LAYERS + 2 * i + 2)
                dve.scalar_tensor_tensor(state[s][:, :], diff[s][:, :], 0.5, new[s][:, :], ALU.mult, ALU.add
                                         ).then_inc(state_ready[s], 1)

            def norm2(s, t):
                dve.wait_ge(state_turned[s], t * LAYERS + LAYERS)
                dve.tensor_tensor(later_root[s].y[:, :, :], chunks(bank[s][1][:, :]), spread(nmask[s][:, :]), ALU.mult
                                  ).then_inc(y_ready[s], 1)
                dve.wait_ge(y_ready[s], t * SUMMED + 2)
                dve.tensor_tensor(later_root[s].y[:, :, :], later_root[s].y[:, :, :], x1[s][:, :, :], ALU.add).then_inc(y_ready[s], 1)
                later_norm(s, t, NORM2, 3)

            def apply2(s, t):
                apply(later_root[s], rooted(t, NORM2), x2[s], x2_ready[s])

            def mask(s, t):
                dve.wait_ge(adj_loaded[s], t * DMA + DMA)
                dve.tensor_scalar(far[:, :, :], adj_s[s][:, :, :], 1.0, -MASK, ALU.subtract, ALU.mult
                                  ).then_inc(far_ready[s], 1)

            def qkv(s, t):
                for tensor, bias in ((0, bqn[:, 0:1]), (1, bqk[:, 1:2])):
                    dve.wait_ge(high_ready[s], t * 2 + tensor + 1)
                    dve.scalar_tensor_tensor(parts[:, LOW[tensor], :], bank[s][1 + tensor][:, :], bias,
                                             parts[:, HIGH[tensor], :].bitcast(F32), ALU.add, ALU.subtract
                                             ).then_inc(low_ready[s], 1)
                dve.wait_ge(qkv_done[s], t * 3 + 3)
                dve.tensor_tensor(vals[s][:, :, :], chunks(bank[s][3][:, :]), rows_of(bv_s[:, :]), ALU.add
                                  ).then_inc(vals_ready[s], 1)

            def degree(s, t):
                dve.wait_ge(deg3_ready[s], t + 1)
                r, tick = later_root[s], t * TICKS + TICK_BASE[DEGREE]
                dve.tensor_copy(r.ve[:, :], deg3[s][:, :]).then_inc(r.tick, 1)
                dve.wait_ge(r.tick, tick + 1)
                seed_root(r, tick + 1)

            def score(s, t, u):
                if u == 0:
                    dve.wait_ge(far_ready[s], t + 1)
                    dve.wait_ge(later_root[s].newton, rooted(t, DEGREE))
                    dve.tensor_copy(d3[s][:, :], later_root[s].root[:, :]).then_inc(d3_ready[s], 1)
                dve.wait_ge(scored[s], t * UNITS + u + 1)
                if u >= 2:
                    dve.wait_ge(prob_ready[s], t * UNITS + u - 1)
                stand_alone()
                dve.tensor_tensor_reduce(masked[u % 2][:, :], bank[s][1 + u % 2][:, :], far[:, u // HEADS, :],
                                         1.0, 3.0e38, ALU.add, ALU.min, low[s][:, u:u + 1]
                                         ).then_inc(masked_ready[s], 1)

            def sums(s, t, c):
                dve.wait_ge(prob_ready[s], t * UNITS + HEADS * c + HEADS)
                dve.reciprocal(einv[s][:, :], esum[s][:, HEADS * c:HEADS * c + HEADS]).then_inc(rsum_ready[s], 1)
                dve.wait_ge(rsum_ready[s], t * 2 * CHUNKS + 2 * c + 1)
                dve.tensor_copy(rwide[s][:, :, :], spread(einv[s][:, :], HEAD)).then_inc(rsum_ready[s], 1)

            def mix(s, t, c):
                dve.wait_ge(rsumt_ready[s], t * CHUNKS + c + 1)
                dve.tensor_tensor(ocol[s][:, c * P:c * P + P], bank[s][0][:, 0:P], rsumt[s][:, :], ALU.mult
                                  ).then_inc(ocol_ready[s], 1)

            def merge(s, t):
                dve.wait_ge(merged[s], t + 1)
                dve.wait_ge(xb_ready[s], t * 2 + 1)
                dve.tensor_tensor(later_root[s].y[:, :, :], chunks(bank[s][2][:, :]), xb[s][:, :, :], ALU.add
                                  ).then_inc(y_ready[s], 1)
                later_norm(s, t, NORM3, 4)

            def apply3(s, t):
                apply(later_root[s], rooted(t, NORM3), x3[s], x3_ready[s])

            def support(s, t):
                dve.wait_ge(supported[s], t + 1)
                dve.wait_ge(d3_ready[s], t + 1)
                dve.tensor_tensor(supp[:, :, :], chunks(bank[s][0][:, :]), spread(d3[s][:, :]), ALU.mult
                                  ).then_inc(supp_ready[s], 1)

            def spread3(s, t, n):
                if n < CHUNKS - 1:
                    return
                dve.wait_ge(spread_done[s], t + 1)
                dve.tensor_tensor(later_root[s].y[:, :, :], chunks(bank[s][3][:, :]), spread(d3[s][:, :]), ALU.mult
                                  ).then_inc(y_ready[s], 1)
                dve.wait_ge(y_ready[s], t * SUMMED + 5)
                dve.wait_ge(xb_ready[s], t * 2 + 2)
                dve.tensor_tensor(later_root[s].y[:, :, :], later_root[s].y[:, :, :], xb[s][:, :, :], ALU.add).then_inc(y_ready[s], 1)
                later_norm(s, t, NORM4, 6)

            def apply4(s, t):
                dve.wait_ge(stored[s], t * DMA + DMA)
                apply(later_root[s], rooted(t, NORM4), y4[s], y4_ready[s])

            run_phases(dve, {
                "norm1": norm1, "apply1": apply1, "gates_sum": gates_sum, "update": update, "norm2": norm2,
                "apply2": apply2, "mask": mask, "qkv": qkv, "degree": degree, "score": score, "sums": sums,
                "mix": mix, "merge": merge, "apply3": apply3, "support": support, "spread": spread3, "apply4": apply4,
            })

        @block.gpsimd
        def _(pool):
            pool.memset(ident[:, :], 0.0).then_inc(ident_zeroed, 1)
            pool.memset(c15[:, :], 1.5)
            pool.wait_ge(ident_zeroed, 1)
            pool.affine_select(out=ident[:, :], in_=ident[:, :], compare_op=ALU.not_equal, fill=1.0, base=0,
                               pattern=[[-1, P]], channel_multiplier=1).then_inc(consts_ready, 1)
            pool.wait_ge(w_loaded, DMA * WEIGHT_LOADS)

            def newton_root(r, seeds, at):
                pool.wait_ge(r.seeded, seeds)
                for step in range(NEWTON_STEPS):
                    if step:
                        pool.wait_ge(r.newton, at + step)
                    out_, a, b, op = [
                        (r.sq, r.root, r.root, ALU.mult), (r.sq, r.sq, r.vh, ALU.mult),
                        (r.sq, r.sq, c15, ALU.add), (r.root, r.root, r.sq, ALU.mult)][step % 4]
                    pool.tensor_tensor(out_[:, :], a[:, :], b[:, :], op).then_inc(r.newton, 1)

            def later_newton(s, t, k):
                newton_root(later_root[s], t * 2 * ROOTS + 2 * k + 2, t * NEWTON_STEPS * ROOTS + NEWTON_STEPS * k)

            def diagonal(tile):
                blocks = tile[:, :, :].rearrange("p c (d m) -> p (c d) m", d=CHUNKS)
                return blocks[:, 0:CHUNKS * CHUNKS:CHUNKS + 1, :]

            def add_self(tile):
                return pool.tensor_tensor(diagonal(tile), diagonal(tile),
                                          ident[:, :].unsqueeze(1).broadcast_to([P, CHUNKS, P]), ALU.add)

            def norm1(s, t):
                newton_root(first_root[s], t * 2 + 2, t * NEWTON_STEPS)

            def norm2(s, t):
                later_newton(s, t, NORM2)

            def degree(s, t):
                pool.wait_ge(aggregated[s], t * LAYERS + LAYERS)
                pool.wait_ge(far_ready[s], t + 1)
                add_self(adj_s[s]).then_inc(self_added[s], 1)
                later_newton(s, t, DEGREE)
                pool.wait_ge(x2_ready[s], t + 1)
                pool.wait_ge(y_ready[s], t * SUMMED + 1)
                pool.tensor_tensor(xb[s][:, :, :], x2[s][:, :, :], rows_of(bo_s[:, :]), ALU.add).then_inc(xb_ready[s], 1)
                pool.wait_ge(adjt_loaded[s], t * DMA + DMA)
                add_self(adjt_s[s]).then_inc(selft_added[s], 1)

            def merge(s, t):
                later_newton(s, t, NORM3)

            def apply3(s, t):
                pool.wait_ge(x3_ready[s], t + 1)
                pool.tensor_tensor(xb[s][:, :, :], x3[s][:, :, :], rows_of(b3_s[:, :]), ALU.add).then_inc(xb_ready[s], 1)

            def spread3(s, t, n):
                if n < CHUNKS - 1:
                    return
                later_newton(s, t, NORM4)

            run_phases(pool, {"norm1": norm1, "norm2": norm2, "degree": degree, "merge": merge,
                              "apply3": apply3, "spread": spread3})


def kernel(x, adj, nodemask, L0_gnn_W_msg, L0_gnn_W_upd, L1_gnn_weight, L1_gnn_w_ih, L1_gnn_w_hh, L1_gnn_b_ih,
           L1_gnn_b_hh, L2_gnn_Wq, L2_gnn_bq, L2_gnn_Wk, L2_gnn_bk, L2_gnn_Wv, L2_gnn_bv, L2_gnn_Wo, L2_gnn_bo,
           L3_gnn_weight, L3_gnn_bias):
    import numpy as np
    import concourse.bacc as bacc
    from concourse.bass_utils import run_bass_kernel_spmd

    def turned(a):
        return np.swapaxes(np.asarray(a), -1, -2)

    def per_feature(a):
        return np.asarray(a).reshape(LAYERS, 3, FEATS).transpose(2, 0, 1)

    given = {
        "x_columns": turned(x), "adj": adj, "adj_t": turned(adj), "node_mask": turned(np.asarray(nodemask).reshape(GRAPHS, CHUNKS, P)),
        "w_msg_t": turned(L0_gnn_W_msg), "w_upd": L0_gnn_W_upd,
        "weight_t": turned(L1_gnn_weight), "w_ih_t": turned(L1_gnn_w_ih), "w_hh_t": turned(L1_gnn_w_hh),
        "b_ih": per_feature(L1_gnn_b_ih), "b_hh": per_feature(L1_gnn_b_hh),
        "wq": L2_gnn_Wq, "bq": np.asarray(L2_gnn_bq).reshape(FEATS, 1), "wk": L2_gnn_Wk, "bk": np.asarray(L2_gnn_bk).reshape(FEATS, 1), "wv": L2_gnn_Wv, "bv": L2_gnn_bv,
        "wo": L2_gnn_Wo, "bo": L2_gnn_bo, "w3": L3_gnn_weight, "b3": L3_gnn_bias,
    }
    nc = bacc.Bacc("TRN2", target_bir_lowering=False, num_devices=1)
    arrays, args = {}, {}
    for name, a in given.items():
        a = np.ascontiguousarray(a)
        arrays[f"in_{name}"] = a
        args[name] = nc.dram_tensor(f"in_{name}", a.shape, mybir.dt.from_np(a.dtype), kind="ExternalInput").ap()
    out = nc.dram_tensor("out", (GRAPHS, NODES, FEATS), F32, kind="ExternalOutput").ap()
    nc.disable_value_cache = True
    graph_layers(nc, **args, out=out)
    r = run_bass_kernel_spmd(nc, [arrays], core_ids=[0])
    return r.results[0]["out"]
```

```python
from collections import namedtuple
from contextlib import ExitStack

import concourse.bass as bass
from concourse import mybir

F32 = mybir.dt.float32
F32R = mybir.dt.float32r
I32 = mybir.dt.int32
ALU = mybir.AluOpType
ACT = mybir.ActivationFunctionType

GRAPHS, NODES, FEATS = 16, 512, 128
P = 128
CHUNKS = NODES // P
LAYERS = 4
HEADS = 4
HEAD = FEATS // HEADS
UNITS = CHUNKS * HEADS
STRANDS = 2
TURNS = GRAPHS // STRANDS
LN_EPS = 1e-5
MASK = 1e9
SCORE_SCALE = float(HEAD) ** -0.5
DMA = 16

NORM2, DEGREE, NORM3, NORM4 = range(4)
ROOTS = 4
NEWTON_ROUNDS = 3
NEWTON_STEPS = 4 * NEWTON_ROUNDS
HELD = [1.0] + [0.5] * (LAYERS - 1)
SEED = 0x5F3759DF
NORM_TICKS = 4
ROOT_TICKS = [NORM_TICKS, 1, NORM_TICKS, NORM_TICKS]
TICK_BASE = [sum(ROOT_TICKS[:k]) for k in range(ROOTS)]
TICKS = sum(ROOT_TICKS)
COMBINED = 9
SUMMED = 5
Root = namedtuple("Root", "y stats mv ve vh bits root sq tick seeded newton")
Q_LOW, Q_HIGH, K_HIGH, K_LOW = range(4)
PRODUCTS = [(Q_HIGH, K_HIGH), (Q_HIGH, K_LOW), (Q_LOW, K_HIGH), (Q_LOW, K_LOW)]
HIGH, LOW = (Q_HIGH, K_HIGH), (Q_LOW, K_LOW)
STACKS = len(PRODUCTS) * HEADS

FIRST = [("turn1",)]
for i in range(LAYERS):
    early = [("gates_state", i, 0)]
    FIRST += early if i else []
    FIRST += [("aggregate", i, c) for c in range(CHUNKS)]
    FIRST += [] if i else early
    FIRST += [("gates_state", i, gate) for gate in (1, 2)]
    FIRST += [("gates_sum", i, gate) for gate in range(3)]
    FIRST += [("update", i), ("turn_state", i)]
FIRST += [("norm2",), ("apply2",)]

LAYER0 = [("project",)] + [("message", c) for c in range(CHUNKS)] + [("receive", 0), ("receive", 1)]
LAYER0 += [("norm1", part) for part in range(4)] + [("apply1",)]
SECOND = """
    mask:0 mask:1 mask:2 turn2 qkv:0 qkv:1 qkv:2 mask:3 degree:0 degree:1 degree:2 degree:3 score:0 score:1
    weights:0 score:2 weights:1 score:3 weights:2 score:4 weights:3 score:5 weights:4 score:6 sums:0
    weights:5 score:7 mix:0 weights:6 score:8 weights:7 score:9 weights:8 score:10 sums:1 weights:9
    score:11 mix:1 weights:10 score:12 weights:11 score:13 weights:12 score:14 sums:2 weights:13 score:15
    mix:2 next:project weights:14 weights:15 sums:3 next:message:0 mix:3 next:message:1 next:message:2
    merge next:message:3 next:receive:0 next:receive:1 next:norm1:0 next:norm1:1 next:norm1:2 next:norm1:3
    next:apply1 apply3 turn3 support spread:0 spread:1 spread:2 spread:3 apply4
""".split()
SECOND = [tuple(int(a) if a.isdigit() else a for a in step.split(":")) for step in SECOND]

BEHIND = [
    1,
    0, 0, 0, 1, 0, 2, 2, 0, 0, 0, 2, 3,
    1, 0, 0, 0, 0, 0, 0, 2, 0, 11, 4, 0,
    3, 0, 2, 6, 2, 0, 2, 6, 2, 0, 5, 0,
    8, 0, 0, 1, 0, 0, 0, 0, 0, 0, 2, 0,
    4, 1,
]
assert sum(BEHIND) == len(SECOND)


def phase_order():
    order, at = [], 0
    for step, n in zip(FIRST, BEHIND):
        order += [(0, step)] + [(1, x) for x in SECOND[at:at + n]]
        at += n
    return order + [(1, x) for x in SECOND[at:]]


PHASE = phase_order()


def walk(steps, first, second):
    for half, (name, *arg) in PHASE:
        if first is None and half == 0 or second is None and half == 1:
            continue
        s, t = (first, second)[half]
        if name == "next":
            if not more(t):
                continue
            t, name, arg = t + 1, arg[0], arg[1:]
        elif isinstance(t, int) and t < 0:
            continue
        if name in steps:
            steps[name](s, t, *arg)


def more(t):
    return not isinstance(t, int) or t + 1 < TURNS


def follows(t):
    return not isinstance(t, int) or t > 0


def run_phases(engine, steps):
    for name, *arg in LAYER0:
        if name in steps:
            steps[name](0, 0, *arg)
    if "fuse" in steps:
        steps["fuse"]()
    walk(steps, (0, 0), (1, -1))
    with engine.Fori(0, TURNS - 1) as t:
        walk(steps, (1, t), (0, t))
        walk(steps, (0, t + 1), (1, t))
    walk(steps, (1, TURNS - 1), (0, TURNS - 1))
    walk(steps, None, (1, TURNS - 1))


def graph_layers(nc, x_columns, adj, adj_t, node_mask, w_msg_t, w_upd, weight_t, w_ih_t, w_hh_t, b_ih, b_hh,
                 wq, bq, wk, bk, wv, bv, wo, bo, w3, b3, out):
    ctx = ExitStack()
    with ctx:
        def sb(name, shape, dt=F32):
            return ctx.enter_context(nc.sbuf_tensor(name, shape, dt))

        def pair(name, shape, dt=F32):
            return [sb(f"{name}{s}", shape, dt) for s in range(STRANDS)]

        def sem(name):
            return ctx.enter_context(nc.semaphore(name))

        def sems(name):
            return [sem(f"{name}{s}") for s in range(STRANDS)]

        ident = sb("ident", [P, P])
        c15 = sb("c15", [P, CHUNKS])
        wmt = sb("wmt", [P, 2 * FEATS])
        wu = sb("wu", [P, 2, FEATS])
        w0 = sb("w0", [P, 3, FEATS])
        wt = sb("wt", [P, LAYERS, FEATS])
        wih = sb("wih", [P, LAYERS, 3 * FEATS])
        wwi = sb("wwi", [P, LAYERS, 3 * FEATS])
        whh = sb("whh", [P, LAYERS, 3 * FEATS])
        bi = sb("bi", [P, LAYERS, 3])
        bh = sb("bh", [P, LAYERS, 3])
        brz = sb("brz", [P, LAYERS, 3])
        bhn = sb("bhn", [P, LAYERS, 1])
        wqk = sb("wqk", [P, 2, FEATS])
        bqk = sb("bqk", [P, 2])
        wqn = sb("wqn", [P, FEATS])
        bqn = sb("bqn", [P, 1])
        wv_s = sb("wv_s", [P, FEATS])
        wo_s = sb("wo_s", [P, FEATS])
        w3_s = sb("w3_s", [P, FEATS])
        bv_s = sb("bv_s", [P, FEATS])
        bo_s = sb("bo_s", [P, FEATS])
        b3_s = sb("b3_s", [P, FEATS])

        adj_s = pair("adj_s", [P, CHUNKS, NODES])
        adjt_s = pair("adjt_s", [P, CHUNKS, NODES])
        xcol = pair("xcol", [P, NODES])
        nmask = pair("nmask", [P, CHUNKS])
        mine = sb("mine", [P, CHUNKS, FEATS])
        sent = pair("sent", [P, CHUNKS, FEATS + 1])
        deg = pair("deg", [P, CHUNKS])
        has = pair("has", [P, CHUNKS])
        inv = pair("inv", [P, CHUNKS])
        minv = pair("minv", [P, CHUNKS])
        deg3 = pair("deg3", [P, CHUNKS])
        d3 = pair("d3", [P, CHUNKS])
        x1 = pair("x1", [P, CHUNKS, FEATS])
        state = pair("state", [P, NODES])
        state_rows = pair("state_rows", [P, CHUNKS, FEATS])
        aggr = pair("aggr", [P, NODES])
        cand = pair("cand", [P, NODES])
        reset = pair("reset", [P, NODES])
        keep = pair("keep", [P, NODES])
        new = pair("new", [P, NODES])
        kept = pair("kept", [P, NODES])
        x2 = pair("x2", [P, CHUNKS, FEATS])
        x3 = pair("x3", [P, CHUNKS, FEATS])
        xb = pair("xb", [P, CHUNKS, FEATS])
        xturn = pair("xturn", [P, NODES])
        vals = pair("vals", [P, CHUNKS, FEATS])
        low = pair("low", [P, UNITS])
        esum = pair("esum", [P, UNITS])
        einv = pair("einv", [P, HEADS])
        rwide = pair("rwide", [P, HEADS, HEAD])
        rsumt = pair("rsumt", [P, P])
        ocol = pair("ocol", [P, NODES])
        y4 = pair("y4", [P, CHUNKS, FEATS])

        def root_of(name):
            tiles = [pair(name + "_y", [P, CHUNKS, FEATS]), pair(name + "_stats", [P, CHUNKS, 6]),
                     pair(name + "_mv", [P, CHUNKS, 2]), pair(name + "_ve", [P, CHUNKS]),
                     pair(name + "_vh", [P, CHUNKS]), pair(name + "_bits", [P, CHUNKS], I32),
                     pair(name + "_root", [P, CHUNKS]), pair(name + "_sq", [P, CHUNKS])]
            chains = [sems(name + "_tick"), sems(name + "_seeded"), sems(name + "_newton")]
            return [Root(*parts_of) for parts_of in zip(*tiles, *chains)]

        first_root = root_of("first")
        later_root = root_of("later")

        supp = sb("supp", [P, CHUNKS, FEATS])
        far = sb("far", [P, CHUNKS, NODES])
        parts = sb("parts", [P, 4, NODES], F32R)
        stack = sb("stack", [P, 2, HEADS, NODES], F32R)
        masked = [sb(f"masked{b}", [P, NODES]) for b in range(2)]
        prob = [sb(f"prob{b}", [P, NODES]) for b in range(2)]
        prob_t = [sb(f"prob_t{b}", [P, CHUNKS, HEADS, P]) for b in range(2)]

        bank = [[ctx.enter_context(nc.psum_tensor(f"bank{s}{b}", [P, NODES], F32)) for b in range(4)]
                for s in range(STRANDS)]

        def chunks(ap):
            return ap.rearrange("p (c f) -> p c f", c=CHUNKS)

        def spread(ap, n=FEATS):
            return ap.unsqueeze(2).broadcast_to([P, ap.shape[1], n])

        def rows_of(ap):
            return ap.unsqueeze(1).broadcast_to([P, CHUNKS, FEATS])

        w0_loaded = sem("w0_loaded")
        w_loaded = sem("w_loaded")
        bias_summed = sem("bias_summed")
        bias_ready = sem("bias_ready")
        waited = sem("waited")
        ident_zeroed = sem("ident_zeroed")
        consts_ready = sem("consts_ready")
        fused0_done = sem("fused0_done")
        w0_ready = sem("w0_ready")
        fused_done = sem("fused_done")
        w_ready = sem("w_ready")
        x_loaded = sems("x_loaded")
        adj_loaded = sems("adj_loaded")
        adjt_loaded = sems("adjt_loaded")
        projected = sems("projected")
        sent_ready = sems("sent_ready")
        messages_done = sems("messages_done")
        received = sems("received")
        combined = sems("combined")
        x1_ready = sems("x1_ready")
        x1_turned = sems("x1_turned")
        state0_ready = sems("state0_ready")
        aggregated = sems("aggregated")
        aggr_ready = sems("aggr_ready")
        hn_done = sems("hn_done")
        r_done = sems("r_done")
        xn_done = sems("xn_done")
        z_done = sems("z_done")
        hn_ready = sems("hn_ready")
        reset_ready = sems("reset_ready")
        gated = sems("gated")
        cand_ready = sems("cand_ready")
        new_ready = sems("new_ready")
        keep_ready = sems("keep_ready")
        kept_ready = sems("kept_ready")
        state_ready = sems("state_ready")
        state_turned = sems("state_turned")
        rows_ready = sems("rows_ready")
        y_ready = sems("y_ready")
        x2_ready = sems("x2_ready")
        x2_turned = sems("x2_turned")
        x2col_ready = sems("x2col_ready")
        qkv_done = sems("qkv_done")
        high_ready = sems("high_ready")
        low_ready = sems("low_ready")
        vals_ready = sems("vals_ready")
        stacked = sems("stacked")
        far_ready = sems("far_ready")
        self_added = sems("self_added")
        selft_added = sems("selft_added")
        deg3_ready = sems("deg3_ready")
        scored = sems("scored")
        masked_ready = sems("masked_ready")
        prob_ready = sems("prob_ready")
        prob_turned = sems("prob_turned")
        probt_ready = sems("probt_ready")
        mixed = sems("mixed")
        rsum_ready = sems("rsum_ready")
        rsumt_ready = sems("rsumt_ready")
        ocol_ready = sems("ocol_ready")
        xb_ready = sems("xb_ready")
        merged = sems("merged")
        x3_ready = sems("x3_ready")
        x3_turned = sems("x3_turned")
        x3col_ready = sems("x3col_ready")
        supported = sems("supported")
        supp_ready = sems("supp_ready")
        spread_done = sems("spread_done")
        y4_ready = sems("y4_ready")
        centred1 = sems("centred1")
        centred4 = sems("centred4")
        stored = sems("stored")

        WEIGHT_LOADS = 15
        block = ctx.enter_context(nc.Block())

        @block.sync
        def _(sp):
            def load_x(s, t):
                sp.dma_start(xcol[s][:, :], x_columns[t * STRANDS + s]).then_inc(x_loaded[s], DMA)
                sp.dma_start(nmask[s][:, :], node_mask[t * STRANDS + s]
                             ).then_inc(x_loaded[s], DMA)

            def load_adj(s, t):
                sp.dma_start(adj_s[s][:, :, :], adj[t * STRANDS + s].rearrange("(c p) m -> p c m", p=P)
                             ).then_inc(adj_loaded[s], DMA)

            def load_adjt(s, t):
                sp.dma_start(adjt_s[s][:, :, :], adj_t[t * STRANDS + s].rearrange("(c p) m -> p c m", p=P)
                             ).then_inc(adjt_loaded[s], DMA)

            load_x(0, 0)
            for tile, src in (
                (wmt[:, :], w_msg_t), (wu[:, :, :], w_upd.rearrange("(h k) n -> k h n", h=2)),
            ):
                sp.dma_start(tile, src).then_inc(w0_loaded, DMA)
            load_adj(0, 0)
            for tile, src in (
                (wt[:, :, :], weight_t.rearrange("l d c -> d l c")),
                (wih[:, :, :], w_ih_t.rearrange("l d g -> d l g")),
                (whh[:, :, :], w_hh_t.rearrange("l d g -> d l g")),
                (bi[:, :, :], b_ih), (bh[:, :, :], b_hh),
                (wqk[:, 0, :], wq), (wqk[:, 1, :], wk),
                (bqk[:, 0:1], bq), (bqk[:, 1:2], bk),
                (wv_s[:, :], wv), (wo_s[:, :], wo), (w3_s[:, :], w3),
                (bv_s[:, :], bv.partition_broadcast(P)), (bo_s[:, :], bo.partition_broadcast(P)),
                (b3_s[:, :], b3.partition_broadcast(P)),
            ):
                sp.dma_start(tile, src).then_inc(w_loaded, DMA)
            load_adjt(0, 0)
            load_x(1, 0)
            load_adj(1, 0)
            load_adjt(1, 0)

            def qkv(s, t, tensor):
                if tensor < 2:
                    return
                sp.wait_ge(high_ready[s], t * 2 + 2)
                sp.wait_ge(low_ready[s], t * 2 + 2)
                for h in range(HEADS):
                    rows = slice(HEAD * h, HEAD * h + HEAD)
                    for quadrant, (q, k) in enumerate(PRODUCTS):
                        sp.dma_start(stack[HEAD * quadrant:HEAD * quadrant + HEAD, :, h, :].bitcast(F32),
                                     parts[rows, q:k + 1:k - q, :].bitcast(F32)).then_inc(stacked[s], DMA)

            def degree(s, t, c):
                if more(t) and c == CHUNKS - 1:
                    sp.wait_ge(x2_ready[s], t + 1)
                    load_x(s, t + 1)
                    sp.wait_ge(deg3_ready[s], t * CHUNKS + CHUNKS)
                    load_adj(s, t + 1)

            def apply4(s, t):
                if more(t):
                    sp.wait_ge(spread_done[s], t + 1)
                    load_adjt(s, t + 1)
                sp.wait_ge(y4_ready[s], t + 2)
                sp.dma_start(out[t * STRANDS + s].rearrange("(c p) f -> p c f", p=P), y4[s][:, :, :]
                             ).then_inc(stored[s], DMA)

            run_phases(sp, {"qkv": qkv, "degree": degree, "apply4": apply4})
            for s in range(STRANDS):
                sp.wait_ge(stored[s], DMA * TURNS + DMA)

        @block.tensor
        def _(pe):
            pe.wait_ge(w0_loaded, 2 * DMA)
            for h in range(2):
                mm = pe.matmul(bank[1][0][:, h * FEATS:h * FEATS + FEATS], wmt[:, h * FEATS:h * FEATS + FEATS],
                               wu[:, 1, :], start=(h == 0), stop=(h == 1), skip_group_check=True)
            mm.then_inc(fused0_done, 1)
            pe.wait_ge(consts_ready, 3)
            pe.wait_ge(w0_ready, 3)

            def fuse():
                pe.wait_ge(w_loaded, DMA * WEIGHT_LOADS)
                for i in range(LAYERS):
                    last = pe.matmul(bank[1][i][:, 0:3 * FEATS], wt[:, i, :], wih[:, i, :], start=True, stop=True)
                last.then_inc(fused_done, 1)
                pe.wait_ge(w_ready, LAYERS)
                pe.wait_ge(bias_ready, 5)

            def by_rows(dst, columns, w):
                for c in range(CHUNKS):
                    mm = pe.matmul(dst[:, c * P:c * P + P], columns[:, c * P:c * P + P], w,
                                   start=(c == 0), stop=(c == CHUNKS - 1), skip_group_check=True)
                return mm

            def project(s, t):
                pe.wait_ge(x_loaded[s], t * 2 * DMA + 2 * DMA)
                if follows(t):
                    pe.wait_ge(masked_ready[s], t * UNITS)
                by_rows(bank[s][1], xcol[s], w0[:, 0, :]).then_inc(projected[s], 1)

            def message(s, t, r):
                if r == 0:
                    pe.wait_ge(sent_ready[s], t + 1)
                    pe.wait_ge(adj_loaded[s], t * DMA + DMA)
                    if follows(t):
                        pe.wait_ge(probt_ready[s], t * UNITS)
                W = FEATS + 1
                dst = bank[s][3][:, r * W:r * W + W] if r < 3 else bank[s][1][:, 0:W]
                for c in range(CHUNKS):
                    mm = pe.matmul(dst, adj_s[s][:, c, r * P:r * P + P], sent[s][:, c, :],
                                   start=(c == 0), stop=(c == CHUNKS - 1), skip_group_check=True)
                if r == CHUNKS - 1:
                    mm.then_inc(messages_done[s], 1)

            def receive(s, t, part):
                if follows(t) and part == 0:
                    pe.wait_ge(ocol_ready[s], t * CHUNKS)
                if follows(t) and part == 1:
                    pe.wait_ge(y_ready[s], t * SUMMED - 1)
                by_rows(bank[s][2 * part], xcol[s], w0[:, 1 + part, :]).then_inc(received[s], 1)

            def turn(dst, rows):
                for c in range(CHUNKS):
                    mm = pe.transpose(dst[:, c * P:c * P + P], rows(c), ident[:, :])
                return mm

            def turn1(s, t):
                pe.wait_ge(x1_ready[s], t + 1)
                turn(bank[s][1], lambda c: x1[s][:, c, :]).then_inc(x1_turned[s], 1)

            def aggregate(s, t, i, c):
                if c == 0 and i == 0:
                    pe.wait_ge(x1_ready[s], t + 1)
                elif c == 0:
                    pe.wait_ge(rows_ready[s], t * (LAYERS - 1) + i)
                rows = x1[s] if i == 0 else state_rows[s]
                mm = pe.matmul(bank[s][0][:, :], rows[:, c, :], adj_s[s][:, c, :],
                               start=(c == 0), stop=(c == CHUNKS - 1))
                if c == CHUNKS - 1:
                    mm.then_inc(aggregated[s], 1)

            R, Z, N = (slice(g * FEATS, g * FEATS + FEATS) for g in range(3))

            def gates_state(s, t, i, gate):
                if i == 0 and gate == 0:
                    pe.wait_ge(state0_ready[s], t + 1)
                    pe.wait_ge(y_ready[s], t * SUMMED + 1)
                if gate == 0:
                    pe.matmul(bank[s][3][:, :], whh[:, i, N], state[s][:, :], start=True, stop=True
                              ).then_inc(hn_done[s], 1)
                else:
                    pe.matmul(bank[s][gate][:, :], whh[:, i, (R, Z)[gate - 1]], state[s][:, :],
                              start=True, stop=False)

            def gates_sum(s, t, i, gate):
                if gate == 0:
                    pe.wait_ge(aggr_ready[s], t * LAYERS + i + 1)
                    pe.matmul(bank[s][1][:, :], wwi[:, i, R], aggr[s][:, :], start=False, stop=True
                              ).then_inc(r_done[s], 1)
                elif gate == 1:
                    pe.matmul(bank[s][0][:, :], wwi[:, i, N], aggr[s][:, :], start=True, stop=True
                              ).then_inc(xn_done[s], 1)
                else:
                    pe.matmul(bank[s][2][:, :], wwi[:, i, Z], aggr[s][:, :], start=False, stop=True
                              ).then_inc(z_done[s], 1)

            def turn_state(s, t, i):
                pe.wait_ge(state_ready[s], t * LAYERS + i + 1)
                turn(bank[s][1], lambda c: state[s][:, c * P:c * P + P]).then_inc(state_turned[s], 1)

            def turn2(s, t):
                pe.wait_ge(x2_ready[s], t + 1)
                turn(bank[s][0], lambda c: x2[s][:, c, :]).then_inc(x2_turned[s], 1)

            def qkv(s, t, tensor):
                if tensor == 0:
                    pe.wait_ge(x2col_ready[s], t + 1)
                if tensor < 2:
                    pe.matmul(bank[s][1 + tensor][:, :], (wqn[:, :], wqk[:, 1, :])[tensor], xturn[s][:, :],
                              start=True, stop=True).then_inc(qkv_done[s], 1)
                else:
                    by_rows(bank[s][3], xturn[s], wv_s[:, :]).then_inc(qkv_done[s], 1)

            def score(s, t, u):
                c, h = u // HEADS, u % HEADS
                if u == 0:
                    pe.wait_ge(stacked[s], t * DMA * STACKS + DMA * STACKS)
                if u >= 2:
                    pe.wait_ge(masked_ready[s], t * UNITS + u - 1)
                pe.matmul(bank[s][1 + u % 2][:, :], stack[:, 0, h, c * P:c * P + P], stack[:, 1, h, :],
                          start=True, stop=True).then_inc(scored[s], 1)

            def weights(s, t, u):
                if u == 0:
                    pe.wait_ge(vals_ready[s], t + 1)
                else:
                    pe.wait_ge(probt_ready[s], t * UNITS + u)
                pe.wait_ge(prob_ready[s], t * UNITS + u + 1)
                turn(bank[s][3], lambda m: prob[u % 2][:, m * P:m * P + P]).then_inc(prob_turned[s], 1)

            def mix(s, t, c):
                pe.wait_ge(probt_ready[s], t * UNITS + HEADS * c + HEADS)
                if c:
                    pe.wait_ge(ocol_ready[s], t * CHUNKS + c)
                for m in range(CHUNKS):
                    for h in range(HEADS):
                        rows = slice(HEAD * h, HEAD * h + HEAD)
                        pe.matmul(bank[s][0][rows, 0:P], vals[s][:, m, rows], prob_t[c % 2][:, m, h, :],
                                  start=(m == 0), stop=(m == CHUNKS - 1), skip_group_check=True)
                pe.wait_ge(rsum_ready[s], t * 2 * CHUNKS + 2 * c + 2)
                pe.transpose(bank[s][0][:, P:2 * P], rwide[s][:, :, :].rearrange("p h d -> p (h d)"), ident[:, :]
                             ).then_inc(mixed[s], 1)

            def merge(s, t):
                pe.wait_ge(ocol_ready[s], t * CHUNKS + CHUNKS)
                pe.wait_ge(masked_ready[s], t * UNITS + UNITS)
                by_rows(bank[s][2], ocol[s], wo_s[:, :]).then_inc(merged[s], 1)

            def turn3(s, t):
                pe.wait_ge(x3_ready[s], t + 1)
                if more(t):
                    pe.wait_ge(combined[s], t * COMBINED + 2 * COMBINED)
                turn(bank[s][1], lambda c: x3[s][:, c, :]).then_inc(x3_turned[s], 1)

            def support(s, t):
                pe.wait_ge(x3col_ready[s], t + 1)
                by_rows(bank[s][0], xturn[s], w3_s[:, :]).then_inc(supported[s], 1)

            def spread3(s, t, n):
                if n == 0:
                    pe.wait_ge(selft_added[s], t + 1)
                    pe.wait_ge(supp_ready[s], t + 1)
                for m in range(CHUNKS):
                    mm = pe.matmul(bank[s][3][:, n * P:n * P + P], adjt_s[s][:, m, n * P:n * P + P],
                                   supp[:, m, :], start=(m == 0), stop=(m == CHUNKS - 1),
                                   skip_group_check=True)
                if n == CHUNKS - 1:
                    mm.then_inc(spread_done[s], 1)

            run_phases(pe, {
                "fuse": fuse,
                "project": project, "message": message, "receive": receive, "turn1": turn1,
                "aggregate": aggregate, "gates_state": gates_state, "gates_sum": gates_sum,
                "turn_state": turn_state, "turn2": turn2, "qkv": qkv, "score": score, "weights": weights,
                "mix": mix, "merge": merge, "turn3": turn3, "support": support, "spread": spread3,
            })

        @block.scalar
        def _(act):
            def fuse():
                act.wait_ge(fused_done, 1)
                for i in range(LAYERS):
                    act.activation(wwi[:, i, :], bank[1][i][:, 0:3 * FEATS], ACT.Copy, scale=HELD[i]
                                   ).then_inc(w_ready, 1)
                act.wait_ge(bias_ready, 5)

            def project(s, t):
                act.wait_ge(projected[s], t + 1)
                act.copy(sent[s][:, :, 0:FEATS], chunks(bank[s][1][:, :])).then_inc(sent_ready[s], 1)

            def turn1(s, t):
                act.wait_ge(x1_turned[s], t + 1)
                act.copy(state[s][:, :], bank[s][1][:, :]).then_inc(state0_ready[s], 1)

            def aggregate(s, t, i, c):
                if c < CHUNKS - 1:
                    return
                act.wait_ge(aggregated[s], t * LAYERS + i + 1)
                act.copy(aggr[s][:, :], bank[s][0][:, :]).then_inc(aggr_ready[s], 1)

            def gates_state(s, t, i, gate):
                if gate:
                    return
                act.wait_ge(hn_done[s], t * LAYERS + i + 1)
                act.activation(cand[s][:, :], bank[s][3][:, :], ACT.Identity, bias=bhn[:, i, :], scale=0.5
                               ).then_inc(hn_ready[s], 1)

            def gates_sum(s, t, i, gate):
                if gate == 2:
                    act.wait_ge(z_done[s], t * LAYERS + i + 1)
                    act.activation(keep[s][:, :], bank[s][2][:, :], ACT.Tanh, bias=brz[:, i, 1:2], scale=0.5
                                   ).then_inc(keep_ready[s], 1)
                if gate:
                    return
                act.wait_ge(r_done[s], t * LAYERS + i + 1)
                act.activation(reset[s][:, :], bank[s][1][:, :], ACT.Tanh, bias=brz[:, i, 0:1], scale=0.5
                               ).then_inc(reset_ready[s], 1)

            def update(s, t, i):
                act.wait_ge(cand_ready[s], t * LAYERS + i + 1)
                act.activation(new[s][:, :], cand[s][:, :], ACT.Tanh, bias=bi[:, i, 2:3], scale=1.0
                               ).then_inc(new_ready[s], 1)

            def turn_state(s, t, i):
                if i < LAYERS - 1:
                    act.wait_ge(state_turned[s], t * LAYERS + i + 1)
                    act.copy(state_rows[s][:, :, :], chunks(bank[s][1][:, :])).then_inc(rows_ready[s], 1)

            def turn2(s, t):
                act.wait_ge(x2_turned[s], t + 1)
                act.copy(xturn[s][:, :], bank[s][0][:, :]).then_inc(x2col_ready[s], 1)

            def qkv(s, t, tensor):
                if tensor < 2:
                    bias = (bqn[:, 0:1], bqk[:, 1:2])[tensor]
                    act.wait_ge(qkv_done[s], t * 3 + tensor + 1)
                    act.activation(parts[:, HIGH[tensor], :], bank[s][1 + tensor][:, :], ACT.Identity,
                                   bias=bias, scale=1.0).then_inc(high_ready[s], 1)

            def degree(s, t, c):
                if c == 0:
                    act.wait_ge(self_added[s], t + 1)
                act.activation(adj_s[s][:, c, :], adj_s[s][:, c, :], ACT.Abs, accum_out=deg3[s][:, c:c + 1]
                               ).then_inc(deg3_ready[s], 1)

            def score(s, t, u):
                act.wait_ge(masked_ready[s], t * UNITS + u + 1)
                if u >= 2:
                    act.wait_ge(prob_turned[s], t * UNITS + u - 1)
                act.activation(prob[u % 2][:, :], masked[u % 2][:, :], ACT.Exp, bias=low[s][:, u:u + 1],
                               scale=-1.0, accum_out=esum[s][:, u:u + 1]).then_inc(prob_ready[s], 1)

            def weights(s, t, u):
                c, h = u // HEADS, u % HEADS
                act.wait_ge(prob_turned[s], t * UNITS + u + 1)
                if c >= 2:
                    act.wait_ge(mixed[s], t * CHUNKS + c - 1)
                act.copy(prob_t[c % 2][:, :, h, :], chunks(bank[s][3][:, :])).then_inc(probt_ready[s], 1)

            def mix(s, t, c):
                act.wait_ge(mixed[s], t * CHUNKS + c + 1)
                act.copy(rsumt[s][:, :], bank[s][0][:, P:2 * P]).then_inc(rsumt_ready[s], 1)

            def turn3(s, t):
                act.wait_ge(x3_turned[s], t + 1)
                act.copy(xturn[s][:, :], bank[s][1][:, :]).then_inc(x3col_ready[s], 1)

            run_phases(act, {
                "fuse": fuse,
                "project": project, "turn1": turn1, "aggregate": aggregate, "gates_state": gates_state,
                "gates_sum": gates_sum, "update": update, "turn_state": turn_state, "turn2": turn2, "qkv": qkv,
                "degree": degree, "score": score, "weights": weights, "mix": mix, "turn3": turn3,
            })

        @block.vector
        def _(dve):
            for s in range(STRANDS):
                dve.sem_inc(y_ready[s], 1)
                dve.sem_inc(stored[s], DMA)
                dve.memset(sent[s][:, :, FEATS:FEATS + 1], 1.0).then_inc(consts_ready, 1)
            dve.wait_ge(w0_loaded, 2 * DMA)
            dve.wait_ge(consts_ready, 3)
            dve.tensor_tensor(w0[:, 2, :], wu[:, 0, :], ident[:, :], ALU.add).then_inc(w0_ready, 1)
            dve.wait_ge(fused0_done, 1)
            dve.tensor_copy(w0[:, 0, :], bank[1][0][:, 0:FEATS]).then_inc(w0_ready, 1)
            dve.tensor_copy(w0[:, 1, :], bank[1][0][:, FEATS:2 * FEATS]).then_inc(w0_ready, 1)
            dve.wait_ge(w_loaded, DMA * WEIGHT_LOADS)
            dve.tensor_tensor(brz[:, :, :], bi[:, :, :], bh[:, :, :], ALU.add).then_inc(bias_summed, 1)
            dve.tensor_scalar(bhn[:, :, :], bh[:, :, 2:3], 0.5, None, ALU.mult).then_inc(bias_ready, 1)
            dve.tensor_scalar(wqn[:, :], wqk[:, 0, :], -SCORE_SCALE, None, ALU.mult).then_inc(bias_ready, 1)
            dve.tensor_scalar(bqn[:, :], bqk[:, 0:1], -SCORE_SCALE, None, ALU.mult).then_inc(bias_ready, 1)
            dve.tensor_scalar(whh[:, 1:, :], whh[:, 1:, :], HELD[1], None, ALU.mult).then_inc(bias_ready, 1)
            dve.wait_ge(bias_summed, 1)
            dve.tensor_scalar(brz[:, :, :], brz[:, :, :], 0.5, None, ALU.mult).then_inc(bias_ready, 1)

            def stand_alone():
                dve.sem_inc(waited, 1)

            def seed_root(r, ve, tick):
                dve.tensor_scalar(r.bits[:, :], ve[:, :].bitcast(I32), 1, None, ALU.logical_shift_right
                                  ).then_inc(r.tick, 1)
                dve.tensor_scalar(r.vh[:, :], ve[:, :], -0.5, None, ALU.mult).then_inc(r.seeded, 1)
                dve.wait_ge(r.tick, tick + 1)
                dve.tensor_scalar(r.root[:, :].bitcast(I32), r.bits[:, :], -1.0, float(SEED), ALU.mult, ALU.add
                                  ).then_inc(r.seeded, 1)

            def norm(r, tick):
                for c in range(CHUNKS):
                    a = dve.bn_stats(r.stats[:, c, :], r.y[:, c, :])
                a.then_inc(r.tick, 1)
                dve.wait_ge(r.tick, tick + 1)
                stand_alone()
                for c in range(CHUNKS):
                    a = dve.bn_aggr(r.mv[:, c, :], r.stats[:, c, :])
                a.then_inc(r.tick, 1)
                dve.wait_ge(r.tick, tick + 2)
                dve.tensor_scalar(r.ve[:, :], r.mv[:, :, 1], LN_EPS, None, ALU.add).then_inc(r.tick, 1)
                dve.wait_ge(r.tick, tick + 3)
                seed_root(r, r.ve, tick + 3)

            def later_norm(s, t, k, summed):
                dve.wait_ge(y_ready[s], t * SUMMED + summed)
                norm(later_root[s], t * TICKS + TICK_BASE[k])

            def apply(r, rooted, dst, ready):
                dve.wait_ge(r.newton, rooted)
                for c in range(CHUNKS):
                    a = dve.tensor_scalar(dst[:, c, :], r.y[:, c, :], r.mv[:, c, 0:1], r.root[:, c:c + 1],
                                          ALU.subtract, ALU.mult)
                a.then_inc(ready, 1)

            def rooted(t, k):
                return t * NEWTON_STEPS * ROOTS + NEWTON_STEPS * (k + 1)

            def norm1(s, t, part):
                W = FEATS + 1
                at = t * COMBINED
                total = first_root[s].y
                sums = bank[s][3][:, 0:3 * W].rearrange("p (c f) -> p c f", c=3)
                last = bank[s][1][:, 0:W]
                if part == 0:
                    dve.wait_ge(messages_done[s], t + 1)
                    dve.tensor_scalar(deg[s][:, 0:3], sums[:, :, FEATS], 1.0, None, ALU.max)
                    dve.tensor_scalar(deg[s][:, 3:4], last[:, FEATS:W], 1.0, None, ALU.max).then_inc(combined[s], 1)
                    dve.tensor_scalar(has[s][:, 0:3], sums[:, :, FEATS], 0.0, None, ALU.is_gt)
                    dve.tensor_scalar(has[s][:, 3:4], last[:, FEATS:W], 0.0, None, ALU.is_gt
                                      ).then_inc(combined[s], 1)
                    dve.wait_ge(combined[s], at + 1)
                    dve.reciprocal(inv[s][:, :], deg[s][:, :]).then_inc(combined[s], 1)
                    dve.wait_ge(combined[s], at + 3)
                    dve.tensor_tensor(minv[s][:, :], inv[s][:, :], has[s][:, :], ALU.mult).then_inc(combined[s], 1)
                    dve.wait_ge(received[s], t * 2 + 1)
                    dve.tensor_tensor(mine[:, :, :], chunks(bank[s][0][:, :]), spread(has[s][:, :]), ALU.mult
                                      ).then_inc(combined[s], 1)
                elif part == 1:
                    if follows(t):
                        dve.wait_ge(x1_ready[s], t)
                    dve.wait_ge(combined[s], at + 4)
                    dve.tensor_tensor(total[:, 0:3, :], sums[:, :, 0:FEATS], spread(minv[s][:, 0:3]), ALU.mult)
                    dve.tensor_tensor(total[:, 3:4, :], last[:, 0:FEATS].unsqueeze(1), spread(minv[s][:, 3:4]),
                                      ALU.mult).then_inc(combined[s], 1)
                elif part == 2:
                    dve.wait_ge(combined[s], at + 6)
                    dve.tensor_tensor(total[:, :, :], total[:, :, :], mine[:, :, :], ALU.add
                                      ).then_inc(combined[s], 1)
                    dve.wait_ge(combined[s], at + 7)
                    dve.wait_ge(received[s], t * 2 + 2)
                    dve.tensor_tensor(total[:, :, :], total[:, :, :], chunks(bank[s][2][:, :]), ALU.add
                                      ).then_inc(combined[s], 2)
                else:
                    dve.wait_ge(combined[s], at + 9)
                    norm(first_root[s], t * NORM_TICKS)

            def gates_sum(s, t, i, gate):
                if gate != 1:
                    return
                dve.wait_ge(hn_ready[s], t * LAYERS + i + 1)
                dve.wait_ge(reset_ready[s], t * LAYERS + i + 1)
                dve.scalar_tensor_tensor(cand[s][:, :], reset[s][:, :], 1.0, cand[s][:, :], ALU.add, ALU.mult
                                         ).then_inc(gated[s], 1)
                dve.wait_ge(gated[s], t * LAYERS + i + 1)
                dve.wait_ge(xn_done[s], t * LAYERS + i + 1)
                dve.tensor_tensor(cand[s][:, :], cand[s][:, :], bank[s][0][:, :], ALU.add).then_inc(cand_ready[s], 1)

            def update(s, t, i):
                dve.wait_ge(keep_ready[s], t * LAYERS + i + 1)
                dve.scalar_tensor_tensor(kept[s][:, :], keep[s][:, :], 1.0, state[s][:, :], ALU.add, ALU.mult
                                         ).then_inc(kept_ready[s], 1)
                dve.wait_ge(new_ready[s], t * LAYERS + i + 1)
                dve.scalar_tensor_tensor(new[s][:, :], keep[s][:, :], 1.0, new[s][:, :], ALU.subtract, ALU.mult
                                         ).then_inc(kept_ready[s], 1)
                dve.wait_ge(kept_ready[s], t * 2 * LAYERS + 2 * i + 2)
                dve.scalar_tensor_tensor(state[s][:, :], kept[s][:, :], HELD[i], new[s][:, :],
                                         ALU.mult, ALU.subtract).then_inc(state_ready[s], 1)

            def norm2(s, t):
                dve.wait_ge(y4_ready[s], t + 1)
                dve.wait_ge(state_turned[s], t * LAYERS + LAYERS)
                dve.tensor_tensor(later_root[s].y[:, :, :], chunks(bank[s][1][:, :]), spread(nmask[s][:, :]), ALU.mult
                                  ).then_inc(y_ready[s], 1)
                dve.wait_ge(y_ready[s], t * SUMMED + 2)
                dve.scalar_tensor_tensor(later_root[s].y[:, :, :], later_root[s].y[:, :, :], HELD[-1],
                                         x1[s][:, :, :], ALU.mult, ALU.add).then_inc(y_ready[s], 1)
                later_norm(s, t, NORM2, 3)

            def apply2(s, t):
                apply(later_root[s], rooted(t, NORM2), x2[s], x2_ready[s])

            def mask(s, t, c):
                dve.wait_ge(adj_loaded[s], t * DMA + DMA)
                dve.tensor_scalar(far[:, c, :], adj_s[s][:, c, :], 1.0, -MASK, ALU.subtract, ALU.mult
                                  ).then_inc(far_ready[s], 1)

            def qkv(s, t, tensor):
                if tensor < 2:
                    bias = (bqn[:, 0:1], bqk[:, 1:2])[tensor]
                    dve.wait_ge(high_ready[s], t * 2 + tensor + 1)
                    dve.scalar_tensor_tensor(parts[:, LOW[tensor], :], bank[s][1 + tensor][:, :], bias,
                                             parts[:, HIGH[tensor], :].bitcast(F32), ALU.add, ALU.subtract
                                             ).then_inc(low_ready[s], 1)
                else:
                    dve.wait_ge(qkv_done[s], t * 3 + 3)
                    dve.tensor_tensor(vals[s][:, :, :], chunks(bank[s][3][:, :]), rows_of(bv_s[:, :]), ALU.add
                                      ).then_inc(vals_ready[s], 1)

            def degree(s, t, c):
                if c < CHUNKS - 1:
                    return
                dve.wait_ge(deg3_ready[s], t * CHUNKS + CHUNKS)
                seed_root(later_root[s], deg3[s], t * TICKS + TICK_BASE[DEGREE])

            def score(s, t, u):
                if u % HEADS == 0:
                    dve.wait_ge(far_ready[s], t * CHUNKS + u // HEADS + 1)
                dve.wait_ge(scored[s], t * UNITS + u + 1)
                if u >= 2:
                    dve.wait_ge(prob_ready[s], t * UNITS + u - 1)
                stand_alone()
                dve.tensor_tensor_reduce(masked[u % 2][:, :], bank[s][1 + u % 2][:, :], far[:, u // HEADS, :],
                                         1.0, 3.0e38, ALU.add, ALU.min, low[s][:, u:u + 1]
                                         ).then_inc(masked_ready[s], 1)

            def sums(s, t, c):
                dve.wait_ge(prob_ready[s], t * UNITS + HEADS * c + HEADS)
                dve.reciprocal(einv[s][:, :], esum[s][:, HEADS * c:HEADS * c + HEADS]).then_inc(rsum_ready[s], 1)
                dve.wait_ge(rsum_ready[s], t * 2 * CHUNKS + 2 * c + 1)
                dve.tensor_copy(rwide[s][:, :, :], spread(einv[s][:, :], HEAD)).then_inc(rsum_ready[s], 1)

            def mix(s, t, c):
                dve.wait_ge(rsumt_ready[s], t * CHUNKS + c + 1)
                dve.tensor_tensor(ocol[s][:, c * P:c * P + P], bank[s][0][:, 0:P], rsumt[s][:, :], ALU.mult
                                  ).then_inc(ocol_ready[s], 1)

            def merge(s, t):
                dve.wait_ge(merged[s], t + 1)
                dve.wait_ge(xb_ready[s], t * 2 + 1)
                dve.tensor_tensor(later_root[s].y[:, :, :], chunks(bank[s][2][:, :]), xb[s][:, :, :], ALU.add
                                  ).then_inc(y_ready[s], 1)
                later_norm(s, t, NORM3, 4)

            def apply3(s, t):
                apply(later_root[s], rooted(t, NORM3), x3[s], x3_ready[s])

            def support(s, t):
                dve.wait_ge(supported[s], t + 1)
                dve.wait_ge(later_root[s].newton, rooted(t, DEGREE))
                dve.tensor_tensor(supp[:, :, :], chunks(bank[s][0][:, :]), spread(d3[s][:, :]), ALU.mult
                                  ).then_inc(supp_ready[s], 1)

            def spread3(s, t, n):
                if n < CHUNKS - 1:
                    return
                dve.wait_ge(spread_done[s], t + 1)
                dve.tensor_tensor(later_root[s].y[:, :, :], chunks(bank[s][3][:, :]), spread(d3[s][:, :]), ALU.mult
                                  ).then_inc(y_ready[s], 1)
                dve.wait_ge(y_ready[s], t * SUMMED + 5)
                dve.wait_ge(xb_ready[s], t * 2 + 2)
                dve.tensor_tensor(later_root[s].y[:, :, :], later_root[s].y[:, :, :], xb[s][:, :, :], ALU.add
                                  ).then_inc(y_ready[s], 1)
                later_norm(s, t, NORM4, 6)

            run_phases(dve, {
                "norm1": norm1, "gates_sum": gates_sum, "update": update, "norm2": norm2,
                "apply2": apply2, "mask": mask, "qkv": qkv, "degree": degree, "score": score, "sums": sums,
                "mix": mix, "merge": merge, "apply3": apply3, "support": support, "spread": spread3,
            })

        @block.gpsimd
        def _(pool):
            pool.memset(ident[:, :], 0.0).then_inc(ident_zeroed, 1)
            pool.memset(c15[:, :], 1.5)
            pool.wait_ge(ident_zeroed, 1)
            pool.affine_select(out=ident[:, :], in_=ident[:, :], compare_op=ALU.not_equal, fill=1.0, base=0,
                               pattern=[[-1, P]], channel_multiplier=1).then_inc(consts_ready, 1)
            pool.wait_ge(w_loaded, DMA * WEIGHT_LOADS)

            for s in range(STRANDS):
                pool.sem_inc(y4_ready[s], 1)

            def newton_root(r, seeds, at, last=None):
                pool.wait_ge(r.seeded, seeds)
                for step in range(NEWTON_STEPS):
                    if step:
                        pool.wait_ge(r.newton, at + step)
                    out_, a, b, op = [
                        (r.sq, r.root, r.root, ALU.mult), (r.sq, r.sq, r.vh, ALU.mult),
                        (r.sq, r.sq, c15, ALU.add), (r.root, r.root, r.sq, ALU.mult)][step % 4]
                    if last is not None and step == NEWTON_STEPS - 1:
                        out_ = last
                    pool.tensor_tensor(out_[:, :], a[:, :], b[:, :], op).then_inc(r.newton, 1)

            def later_newton(s, t, k, last=None):
                newton_root(later_root[s], t * 2 * ROOTS + 2 * k + 2,
                            t * NEWTON_STEPS * ROOTS + NEWTON_STEPS * k, last)

            def apply(r, rooted, centre, count, dst, ready):
                pool.tensor_tensor(r.y[:, :, :], r.y[:, :, :], spread(r.mv[:, :, 0]), ALU.subtract
                                   ).then_inc(centre, 1)
                pool.wait_ge(centre, count)
                pool.wait_ge(r.newton, rooted)
                pool.tensor_tensor(dst[:, :, :], r.y[:, :, :], spread(r.root[:, :]), ALU.mult).then_inc(ready, 1)

            def diagonal(tile):
                blocks = tile[:, :, :].rearrange("p c (d m) -> p (c d) m", d=CHUNKS)
                return blocks[:, 0:CHUNKS * CHUNKS:CHUNKS + 1, :]

            def add_self(tile):
                return pool.tensor_tensor(diagonal(tile), diagonal(tile),
                                          ident[:, :].unsqueeze(1).broadcast_to([P, CHUNKS, P]), ALU.add)

            def norm1(s, t, part):
                if part == 3:
                    newton_root(first_root[s], t * 2 + 2, t * NEWTON_STEPS)

            def norm2(s, t):
                later_newton(s, t, NORM2)

            def degree(s, t, c):
                if c:
                    return
                pool.wait_ge(aggregated[s], t * LAYERS + LAYERS)
                pool.wait_ge(far_ready[s], t * CHUNKS + CHUNKS)
                add_self(adj_s[s]).then_inc(self_added[s], 1)
                later_newton(s, t, DEGREE, d3[s])
                pool.wait_ge(x2_ready[s], t + 1)
                pool.wait_ge(y_ready[s], t * SUMMED + 1)
                pool.tensor_tensor(xb[s][:, :, :], x2[s][:, :, :], rows_of(bo_s[:, :]), ALU.add
                                   ).then_inc(xb_ready[s], 1)
                pool.wait_ge(adjt_loaded[s], t * DMA + DMA)
                add_self(adjt_s[s]).then_inc(selft_added[s], 1)

            def merge(s, t):
                later_newton(s, t, NORM3)

            def apply3(s, t):
                pool.wait_ge(x3_ready[s], t + 1)
                pool.tensor_tensor(xb[s][:, :, :], x3[s][:, :, :], rows_of(b3_s[:, :]), ALU.add
                                   ).then_inc(xb_ready[s], 1)

            def spread3(s, t, n):
                if n == CHUNKS - 1:
                    later_newton(s, t, NORM4)

            def apply1(s, t):
                apply(first_root[s], t * NEWTON_STEPS + NEWTON_STEPS, centred1[s], t + 1, x1[s], x1_ready[s])

            def apply4(s, t):
                pool.wait_ge(stored[s], t * DMA + DMA)
                apply(later_root[s], (t + 1) * NEWTON_STEPS * ROOTS, centred4[s], t + 1, y4[s], y4_ready[s])

            run_phases(pool, {"norm1": norm1, "norm2": norm2, "degree": degree, "merge": merge,
                              "apply3": apply3, "spread": spread3, "apply1": apply1, "apply4": apply4})


def kernel(x, adj, nodemask, L0_gnn_W_msg, L0_gnn_W_upd, L1_gnn_weight, L1_gnn_w_ih, L1_gnn_w_hh, L1_gnn_b_ih,
           L1_gnn_b_hh, L2_gnn_Wq, L2_gnn_bq, L2_gnn_Wk, L2_gnn_bk, L2_gnn_Wv, L2_gnn_bv, L2_gnn_Wo, L2_gnn_bo,
           L3_gnn_weight, L3_gnn_bias):
    import numpy as np
    import concourse.bacc as bacc
    from concourse.bass_utils import run_bass_kernel_spmd

    def turned(a):
        return np.swapaxes(np.asarray(a), -1, -2)

    def per_feature(a):
        return np.asarray(a).reshape(LAYERS, 3, FEATS).transpose(2, 0, 1)

    given = {
        "x_columns": turned(x), "adj": adj, "adj_t": turned(adj),
        "node_mask": turned(np.asarray(nodemask).reshape(GRAPHS, CHUNKS, P)),
        "w_msg_t": turned(L0_gnn_W_msg), "w_upd": L0_gnn_W_upd,
        "weight_t": turned(L1_gnn_weight), "w_ih_t": turned(L1_gnn_w_ih), "w_hh_t": turned(L1_gnn_w_hh),
        "b_ih": per_feature(L1_gnn_b_ih), "b_hh": per_feature(L1_gnn_b_hh),
        "wq": L2_gnn_Wq, "bq": np.asarray(L2_gnn_bq).reshape(FEATS, 1),
        "wk": L2_gnn_Wk, "bk": np.asarray(L2_gnn_bk).reshape(FEATS, 1), "wv": L2_gnn_Wv, "bv": L2_gnn_bv,
        "wo": L2_gnn_Wo, "bo": L2_gnn_bo, "w3": L3_gnn_weight, "b3": L3_gnn_bias,
    }
    nc = bacc.Bacc("TRN2", target_bir_lowering=False, num_devices=1)
    arrays, args = {}, {}
    for name, a in given.items():
        a = np.ascontiguousarray(a)
        arrays[f"in_{name}"] = a
        args[name] = nc.dram_tensor(f"in_{name}", a.shape, mybir.dt.from_np(a.dtype), kind="ExternalInput").ap()
    out = nc.dram_tensor("out", (GRAPHS, NODES, FEATS), F32, kind="ExternalOutput").ap()
    nc.disable_value_cache = True
    graph_layers(nc, **args, out=out)
    r = run_bass_kernel_spmd(nc, [arrays], core_ids=[0])
    return r.results[0]["out"]
```
